# Optimizing a Trainium2 kernel written in Bass

```python
import numpy as np
import jax
import jax.numpy as jnp

def _softmax(x, axis=-1):
    return jax.nn.softmax(x, axis=axis)

def _gelu(x):
    return jax.nn.gelu(x, approximate=True)

def _silu(x):
    return jax.nn.silu(x)

def _sigmoid(x):
    return jax.nn.sigmoid(x)

def _layernorm(x, axis=-1, eps=1e-05):
    m = jnp.mean(x, axis=axis, keepdims=True)
    v = jnp.var(x, axis=axis, keepdims=True)
    return (x - m) / jnp.sqrt(v + eps)

def _scatter_add(tgt, idx, src, axis=0):
    return tgt.at[idx].add(src)

def _segment_sum(src, seg, n):
    return jax.ops.segment_sum(src, seg, n)
kernel_name = 'mk_seq_preln_d1_jaxref_r8_788ef5'

def setup_inputs(seed: int=0):
    np.random.seed(seed)
    _w = jnp.asarray

    def _L0_attn_setup():
        import jax, jax.numpy as jnp
        import numpy as np
        DIM = 256
        N_HEADS = 16
        HEAD_DIM = DIM // N_HEADS
        WINDOW = 32
        B, S = (2, 256)
        key = jax.random.key(seed)
        kx, kq, kk, kv, ko = jax.random.split(key, 5)
        bound = 1.0 / np.sqrt(DIM)
        x = jax.random.normal(kx, (B, S, DIM), dtype=jnp.float32)
        wq = jax.random.uniform(kq, (DIM, DIM), jnp.float32, -bound, bound)
        wk = jax.random.uniform(kk, (DIM, DIM), jnp.float32, -bound, bound)
        wv = jax.random.uniform(kv, (DIM, DIM), jnp.float32, -bound, bound)
        wo = jax.random.uniform(ko, (DIM, DIM), jnp.float32, -bound, bound)
        return {'x': x, 'wq': wq, 'wk': wk, 'wv': wv, 'wo': wo}
    _L0_attn_in = _L0_attn_setup()

    def _L0_ffn_setup():
        import jax, jax.numpy as jnp
        import numpy as np
        HIDDEN = 256
        INTER = 1024
        COMPRESSION = 128.9

        def _n_ctrl(out_size, in_size):
            return max(16, int(out_size * in_size / COMPRESSION))

        def _catmull_rom_grid(n_ctrl, n_samples):
            t = np.linspace(0.0, n_ctrl - 1.0, n_samples, dtype=np.float64)
            i = np.clip(np.floor(t).astype(np.int64), 0, n_ctrl - 2)
            f = (t - i).astype(np.float32)
            idx = np.stack([np.clip(i + k, 0, n_ctrl - 1) for k in (-1, 0, 1, 2)], axis=0)
            return (jnp.asarray(idx.astype(np.int32)), jnp.asarray(f))

        def spline_reconstruct(control_points, out_size, in_size):
            n = out_size * in_size
            idx, f = _catmull_rom_grid(control_points.shape[0], n)
            p0, p1, p2, p3 = (control_points[idx[0]], control_points[idx[1]], control_points[idx[2]], control_points[idx[3]])
            f2 = f * f
            f3 = f2 * f
            w = 0.5 * (2.0 * p1 + (p2 - p0) * f + (2.0 * p0 - 5.0 * p1 + 4.0 * p2 - p3) * f2 + (3.0 * p1 - p0 - 3.0 * p2 + p3) * f3)
            return w.reshape(out_size, in_size)
        key = jax.random.key(seed)
        k0, k1, k2, k3 = jax.random.split(key, 4)
        hidden_states = jax.random.normal(k0, (4, 256, HIDDEN), dtype=jnp.float32)
        gate_cp = jax.random.normal(k1, (_n_ctrl(INTER, HIDDEN),), dtype=jnp.float32) * 0.02
        up_cp = jax.random.normal(k2, (_n_ctrl(INTER, HIDDEN),), dtype=jnp.float32) * 0.02
        down_cp = jax.random.normal(k3, (_n_ctrl(HIDDEN, INTER),), dtype=jnp.float32) * 0.02
        return {'hidden_states': hidden_states, 'gate_cp': gate_cp, 'up_cp': up_cp, 'down_cp': down_cp}
    _L0_ffn_in = _L0_ffn_setup()
    _d = {'L0_attn_x': _L0_attn_in['x'], 'L0_attn_wq': _L0_attn_in['wq'], 'L0_attn_wk': _L0_attn_in['wk'], 'L0_attn_wv': _L0_attn_in['wv'], 'L0_attn_wo': _L0_attn_in['wo'], 'L0_ffn_gate_cp': _L0_ffn_in['gate_cp'], 'L0_ffn_up_cp': _L0_ffn_in['up_cp'], 'L0_ffn_down_cp': _L0_ffn_in['down_cp']}
    _x0 = _d['L0_attn_x']
    _d['L0_attn_x'] = jax.random.normal(jax.random.fold_in(jax.random.key(seed), 1), (16, 256, 256), dtype=_x0.dtype)
    del _x0
    return _d

def reference(L0_attn_x, L0_attn_wq, L0_attn_wk, L0_attn_wv, L0_attn_wo, L0_ffn_gate_cp, L0_ffn_up_cp, L0_ffn_down_cp):

    def _L0_attn_ref(x, wq, wk, wv, wo):
        import jax, jax.numpy as jnp
        import numpy as np
        DIM = 256
        N_HEADS = 16
        HEAD_DIM = DIM // N_HEADS
        WINDOW = 32
        B, S = (2, 256)
        b, s, d = x.shape
        scale = HEAD_DIM ** (-0.5)
        q = (x @ wq.T).reshape(b, s, N_HEADS, HEAD_DIM)
        k = (x @ wk.T).reshape(b, s, N_HEADS, HEAD_DIM)
        v = (x @ wv.T).reshape(b, s, N_HEADS, HEAD_DIM)
        scores = jnp.einsum('bihd,bjhd->bhij', q, k) * scale
        idx = jnp.arange(s)
        mask = idx[None, :] - idx[:, None] > WINDOW // 2
        scores = jnp.where(mask[None, None, :, :], -jnp.inf, scores)
        attn = jax.nn.softmax(scores, axis=-1)
        out = jnp.einsum('bhij,bjhd->bihd', attn, v).reshape(b, s, d)
        return out @ wo.T

    def _L0_ffn_ref(hidden_states, gate_cp, up_cp, down_cp):
        import jax, jax.numpy as jnp
        import numpy as np
        HIDDEN = 256
        INTER = 1024
        COMPRESSION = 128.9

        def _n_ctrl(out_size, in_size):
            return max(16, int(out_size * in_size / COMPRESSION))

        def _catmull_rom_grid(n_ctrl, n_samples):
            t = np.linspace(0.0, n_ctrl - 1.0, n_samples, dtype=np.float64)
            i = np.clip(np.floor(t).astype(np.int64), 0, n_ctrl - 2)
            f = (t - i).astype(np.float32)
            idx = np.stack([np.clip(i + k, 0, n_ctrl - 1) for k in (-1, 0, 1, 2)], axis=0)
            return (jnp.asarray(idx.astype(np.int32)), jnp.asarray(f))

        def spline_reconstruct(control_points, out_size, in_size):
            n = out_size * in_size
            idx, f = _catmull_rom_grid(control_points.shape[0], n)
            p0, p1, p2, p3 = (control_points[idx[0]], control_points[idx[1]], control_points[idx[2]], control_points[idx[3]])
            f2 = f * f
            f3 = f2 * f
            w = 0.5 * (2.0 * p1 + (p2 - p0) * f + (2.0 * p0 - 5.0 * p1 + 4.0 * p2 - p3) * f2 + (3.0 * p1 - p0 - 3.0 * p2 + p3) * f3)
            return w.reshape(out_size, in_size)
        gate_w = spline_reconstruct(gate_cp, INTER, HIDDEN)
        up_w = spline_reconstruct(up_cp, INTER, HIDDEN)
        down_w = spline_reconstruct(down_cp, HIDDEN, INTER)
        gate = jnp.einsum('bsh,ih->bsi', hidden_states, gate_w)
        up = jnp.einsum('bsh,ih->bsi', hidden_states, up_w)
        inter = jax.nn.silu(gate) * up
        return jnp.einsum('bsi,hi->bsh', inter, down_w)
    x = L0_attn_x
    x = x + _L0_attn_ref(_layernorm(x, axis=-1), L0_attn_wq, L0_attn_wk, L0_attn_wv, L0_attn_wo)
    x = x + _L0_ffn_ref(_layernorm(x, axis=-1), L0_ffn_gate_cp, L0_ffn_up_cp, L0_ffn_down_cp)
    return x

_drawn_inputs = setup_inputs


def setup_inputs(seed=0):
    import zlib

    import numpy as np

    out = dict(_drawn_inputs(seed))
    spreads = {}
    factors = {'L0_attn_wq': 4.059, 'L0_attn_wk': 3.93, 'L0_ffn_up_cp': 3.12, 'L0_ffn_down_cp': 3.291}
    for name, (base, spread) in spreads.items():
        noise = np.random.default_rng([zlib.crc32(name.encode()), seed]).standard_normal(out[name].shape)
        drawn = base * np.exp(spread * noise) if base else spread * noise
        out[name] = jnp.asarray(drawn.astype(out[name].dtype))
    for name, factor in factors.items():
        out[name] = (out[name] * factor).astype(out[name].dtype)
    return out
```

```python
from contextlib import ExitStack

import numpy as np

import concourse.bass as bass
from concourse import mybir

F32 = mybir.dt.float32
F32R = mybir.dt.float32r
BF16 = mybir.dt.bfloat16
ALU = mybir.AluOpType
ACT = mybir.ActivationFunctionType
AX = mybir.AxisListType

B, S, D = 16, 256, 256
H, DH = 16, 16
INTER = 1024
WINDOW = 32
AHEAD = WINDOW // 2
EPS = 1e-5
SCALE = DH ** -0.5
NEG = -1e30

SEQS = 2
T = SEQS * S
TURNS = B // SEQS
TT = T // 128
KB = D // 128
IB = INTER // 128
NP = H // 2
NG = H // 4
J1 = 128 - AHEAD
W1 = S - J1
STACK = 64
MROW = 3 * DH

COMPRESSION = 128.9
NW = INTER * D
NC = max(16, int(NW / COMPRESSION))
NI = NC - 1


def spline_grid():
    t = np.linspace(0.0, NC - 1.0, NW, dtype=np.float64)
    i = np.clip(np.floor(t).astype(np.int64), 0, NC - 2)
    f = (t - i).astype(np.float32)
    first = np.searchsorted(i, np.arange(NI))
    return i, f, first, np.append(first[1:], NW) - first


GRID_I, GRID_F, FIRST, COUNT = spline_grid()
LEN = int(COUNT.min())
GI = -(-NI // 128)
assert COUNT.max() == LEN + 1


def fraction_table():
    table = np.zeros((GI * 128, LEN + 1), np.float32)
    for i in range(NI):
        table[i, :COUNT[i]] = GRID_F[FIRST[i]:FIRST[i] + COUNT[i]]
    return np.ascontiguousarray(table.reshape(GI, 128, LEN + 1).transpose(1, 0, 2)).reshape(128, -1)


def spline_runs():
    runs, i = [], 0
    while i < NI:
        n = 1
        while i + n < NI and (i + n) % 128 and FIRST[i + n] - FIRST[i] == LEN * n:
            n += 1
        runs.append((i, n))
        i += n
    return runs


def build(nc, x, wqk, wv, wo, points, fractions, ident, identb, upper, out):
    ctx = ExitStack()
    with ctx:
        def sb(name, shape, dt=F32):
            return ctx.enter_context(nc.sbuf_tensor(name, shape, dt))

        def sem(name):
            return ctx.enter_context(nc.semaphore(name))

        qk_scratch = nc.dram_tensor("qk_scratch", (2, 2 * D, T), F32, kind="Internal").ap()
        w_scratch = nc.dram_tensor("w_scratch", (3, NW), F32, kind="Internal").ap()

        ID = sb("ID", [128, 128])
        IDB = sb("IDB", [128, 128], BF16)
        UP = sb("UP", [128, 128], BF16)
        WQKh = sb("WQKh", [128, KB, 2 * D], F32R)
        WQKl = sb("WQKl", [128, KB, 2 * D], F32R)
        WV = sb("WV", [128, KB, 2 * D], F32R)
        WO = sb("WO", [128, KB, 2 * D], F32R)
        WGUh = sb("WGUh", [128, 2, KB, INTER], F32R)
        WGUl = sb("WGUl", [128, 2, KB, INTER], F32R)
        WD = sb("WD", [128, IB, 2 * D], F32R)
        X = sb("X", [128, TT, D])
        X1 = sb("X1", [128, TT, D])
        Z = sb("Z", [128, TT, D])
        ST = sb("ST", [128, TT, 6])
        MV = sb("MV", [128, TT, 2])
        VE = sb("VE", [128, TT])
        RSTD = sb("RSTD", [128, TT])
        HALF = sb("HALF", [128, TT])
        ZT = sb("ZT", [128, 2, KB, T], F32R)
        YT = sb("YT", [128, 2, KB, T], F32R)
        QKE = sb("QKE", [128, 2, T], F32R)
        QM = sb("QM", [128, NP, 2, T], F32R)
        KS = sb("KS", [128, NP, T], F32R)
        V = sb("V", [128, TT, H, 2, DH])
        M = sb("M", [128, SEQS, 2, H])
        MT = YT[0:H, 0, 0, :]
        P0 = sb("P0", [128, 2, 4, S])
        P1 = sb("P1", [128, 2, 4, W1])
        OT = sb("OT", [128, NG, S])
        R = sb("R", [128, H])
        VC = sb("VC", [128, D])

        with ExitStack() as early:
            FR = early.enter_context(nc.sbuf_tensor("FR", [128, GI, LEN + 1], F32))
            SW = early.enter_context(nc.sbuf_tensor("SW", [128, 3, GI, LEN + 1], F32))
            CP = early.enter_context(nc.sbuf_tensor("CP", [128, 3, 4, GI], F32))
            CO = early.enter_context(nc.sbuf_tensor("CO", [128, 3, 3, GI], F32))
            CT = early.enter_context(nc.sbuf_tensor("CT", [128, 3, GI], F32))
        WN = SW[:, :, :, :].rearrange("p m g s -> p (m g s)")[:, 0:3 * 2 * INTER].rearrange(
            "p (m c) -> p m c", m=3)
        GU = sb("GU", [128, 2, T])
        IN = sb("IN", [128, IB, 2, T], F32R)
        RAW = P0[:, :, :, :].rearrange("p a b c -> p (a b c)")

        bank = [ctx.enter_context(nc.psum_tensor(f"bank{i}", [128, 512], F32)) for i in range(8)]
        S_BANK = bank[0:2]
        AV_BANK = bank[2]
        TURN_BANK = bank[3]
        LIN_BANK = bank[4:8]

        (const_loaded, raw_loaded, points_loaded, w_stored, wn_loaded, x_loaded, qk_stored,
         qm_loaded, ks_loaded, zero_loaded, m_loaded, y_stored) = [sem(n) for n in (
             "const_loaded", "raw_loaded", "points_loaded", "w_stored", "wn_loaded", "x_loaded",
             "qk_stored", "qm_loaded", "ks_loaded", "zero_loaded", "m_loaded", "y_stored")]
        (pre_act, pre_dve, pre_pool, pre_pe, coef_done, lin_start, spline_done) = [sem(n) for n in (
            "pre_act", "pre_dve", "pre_pool", "pre_pe", "coef_done", "lin_start", "spline_done")]
        (pool_on, dve_on, dve_step, var_done, rstd_done, rows_done, turned, turn_high, z_low, o_done, on_low, z2_low,
         lin_done, lin_high, qk_split, v_done, s1_done, max_done, mt_done, st_done, exp_done,
         sel_done, av_done, ot_done, tanh_done, up_done, in_high, in_low, x1_done, y_done) = [
             sem(n) for n in (
                 "pool_on", "dve_on", "dve_step", "var_done", "rstd_done", "rows_done", "turned", "turn_high", "z_low",
                 "o_done", "on_low", "z2_low", "lin_done", "lin_high", "qk_split", "v_done",
                 "s1_done", "max_done", "mt_done", "st_done", "exp_done", "sel_done", "av_done",
                 "ot_done", "tanh_done", "up_done", "in_high", "in_low", "x1_done", "y_done")]

        N_LIN = 4 + TT + TT + 2 * IB + TT
        U_QK, U_V, U_WO, U_GU, U_DN = 0, 4, 4 + TT, 4 + 2 * TT, 4 + 2 * TT + 2 * IB
        N_TURN = KB + SEQS + TT + KB + KB
        T_Z, T_M, T_O, T_ON, T_Z2 = 0, KB, KB + SEQS, KB + SEQS + TT, KB + SEQS + TT + KB
        N_S = SEQS * NP * 2
        N_G = SEQS * NG
        N_HIGH = 4 + 3 * TT
        N_STEP = 4 + TT + TT + IB + TT

        runs = spline_runs()
        extra = [int(i) for i in np.nonzero(COUNT == LEN + 1)[0]]
        N_W_STORES = len(runs) + len(extra)

        def evac_ot(act, t, g):
            act.wait_ge(av_done, 1 + t * N_G + g + 1)
            if g % NG == 0:
                if g == 0:
                    act.wait_ge(turned, 1 + t * N_TURN)
                else:
                    act.wait_ge(turned, 1 + t * N_TURN + T_O + 2)
            nc.scalar.activation(OT[:, g % NG, :], AV_BANK[:, 0:S], ACT.Copy).then_inc(ot_done, 1)

        def spline_bank(u):
            return LIN_BANK[u % 4][:, 0:512] if u < 8 else LIN_BANK[u % 4][:, :].rearrange("p (a n) -> p a n", a=2)

        def spline_part(u, part):
            if u < 8:
                m, kb, half = u // 4, u // 2 % 2, u % 2
                return (WGUh, WGUl)[part][:, m, kb, half * 512:(half + 1) * 512]
            ib = 2 * (u - 8)
            return WD[:, ib:ib + 2, part * D:(part + 1) * D]

        def values(tile, h):
            return V[:, tile, h, :, :].rearrange("p a c -> p (a c)")


        block = ctx.enter_context(nc.Block())

        loop_sems = (x_loaded, qk_stored, qm_loaded, ks_loaded, zero_loaded, m_loaded, y_stored, dve_step,
                     var_done, rstd_done, rows_done, turned, turn_high, z_low, o_done, on_low, z2_low,
                     lin_done, lin_high, qk_split, v_done, s1_done, max_done, mt_done, st_done, exp_done,
                     sel_done, av_done, ot_done, tanh_done, up_done, in_high, in_low, x1_done, y_done)

        @block.sync
        def _(sp):
            for dst, src in ((ID, ident), (IDB, identb), (UP, upper)):
                sp.dma_start(dst[:], src).then_inc(const_loaded, 16)
            sp.dma_start(RAW[:, 0:4 * D].rearrange("p (k n) -> p k n", k=KB),
                         wqk.rearrange("(k p) n -> p k n", p=128)).then_inc(raw_loaded, 16)
            for i, w in ((2, wv), (3, wo)):
                sp.dma_start(RAW[:, i * KB * D:(i + 1) * KB * D].rearrange("p (k n) -> p k n", k=KB),
                             w.rearrange("(k p) n -> p k n", p=128)).then_inc(raw_loaded, 16)
            sp.dma_start(CP[:], points.rearrange("p (m k g) -> p m k g", m=3, k=4)).then_inc(points_loaded, 16)
            sp.dma_start(FR[:], fractions.rearrange("p (g s) -> p g s", g=GI)).then_inc(points_loaded, 16)
            for s in loop_sems:
                sp.sem_inc(s, 1)
            sp.wait_ge(spline_done, 3)
            for i, n in runs:
                g, p = divmod(i, 128)
                a = int(FIRST[i])
                sp.dma_start(w_scratch[:, a:a + n * LEN].rearrange("m (p s) -> p m s", s=LEN),
                             SW[p:p + n, :, g, 0:LEN]).then_inc(w_stored, 16)
            for i in extra:
                g, p = divmod(i, 128)
                a = int(FIRST[i]) + LEN
                sp.dma_start(w_scratch[:, a:a + 1].rearrange("m s -> s m"),
                             SW[p:p + 1, :, g, LEN], allow_slow_non_contiguous=True).then_inc(w_stored, 16)
            sp.wait_ge(w_stored, 16 * N_W_STORES)
            for m in range(2):
                sp.dma_start(WN[:, m, :].rearrange("p (o i) -> p o i", i=D),
                             w_scratch[m, :].rearrange("(o p i) -> p o i", p=128, i=D)).then_inc(wn_loaded, 16)
            sp.dma_start(WN[:, 2, :].rearrange("p (o i) -> p o i", i=INTER),
                         w_scratch[2, :].rearrange("(o p i) -> p o i", p=128, i=INTER)).then_inc(wn_loaded, 16)

            with sp.Fori(0, TURNS) as t:
                sp.wait_ge(x1_done, 1 + t * TT)
                sp.dma_start(X[:], x[bass.ds(t * T, T), :].rearrange("(j p) d -> p j d", p=128)).then_inc(x_loaded, 16)
                for mb in range(4):
                    sp.wait_ge(qk_split, 1 + t * 4 + mb + 1)
                    sp.dma_start(qk_scratch[:, mb * 128:(mb + 1) * 128, :].rearrange("c p t -> p c t"),
                                 QKE[:].bitcast(F32)).then_inc(qk_stored, 16)
                sp.wait_ge(st_done, 1 + t * N_S)
                for which, parts in ((0, (0, 1, 0)), (1, (0, 0, 1))):
                    if which == 0:
                        sp.wait_ge(qk_stored, 1 + t * 64 + 32)
                        sp.wait_ge(pre_pool, 3)
                    else:
                        sp.wait_ge(qk_stored, 1 + t * 64 + 64)
                        sp.wait_ge(pre_pool, 2)
                    for a in range(2):
                        for c, part in enumerate(parts):
                            src = qk_scratch[part, which * D:(which + 1) * D, :].rearrange(
                                "(p a d) t -> a d p t", a=2, d=DH)[a]
                            r = STACK * a + DH * c
                            if which == 0:
                                sp.dma_start(QM[r:r + DH, :, a, :].bitcast(F32), src).then_inc(qm_loaded, 16)
                            else:
                                sp.dma_start(KS[r:r + DH, :, :].bitcast(F32), src).then_inc(ks_loaded, 16)
                for a in range(2):
                    r = STACK * a + MROW
                    z = STACK * (1 - a)
                    sp.dma_start(QM[r:r + 1, :, a, :].bitcast(F32), QM[z:z + 1, :, a, :].bitcast(F32)).then_inc(zero_loaded, 16)
                sp.wait_ge(mt_done, 1 + t * SEQS + SEQS)
                for a in range(2):
                    r = STACK * a + MROW
                    sp.dma_start(QM[r:r + 1, :, a, :].bitcast(F32), MT[a * NP:(a + 1) * NP, :].bitcast(F32)).then_inc(m_loaded, 16)
                sp.wait_ge(y_done, 1 + t * TT + TT)
                sp.dma_start(out[bass.ds(t * T, T), :].rearrange("(j p) d -> p j d", p=128), X1[:]).then_inc(y_stored, 16)
            sp.wait_ge(y_stored, 1 + 16 * TURNS)

        @block.gpsimd
        def _(pool):
            nc.gpsimd.memset(KS[32:64, :, :].bitcast(F32), 1.0).then_inc(pre_pool, 1)
            pool.wait_ge(pre_pool, 1)
            nc.gpsimd.memset(KS[96:128, :, :].bitcast(F32), 1.0).then_inc(pre_pool, 1)
            pool.wait_ge(pre_pool, 2)
            nc.gpsimd.memset(QM[:].bitcast(F32), 0.0).then_inc(pre_pool, 1)
            nc.gpsimd.memset(V[:, :, :, 1, :], 1.0).then_inc(pre_pool, 1)
            nc.gpsimd.memset(HALF[:], -0.5).then_inc(pre_pool, 1)
            pool.wait_ge(pre_pool, 5)
            with pool.Fori(0, TURNS) as t:
                def rstd(n):
                    pool.wait_ge(var_done, 1 + t * 2 + n + 1)
                    if n == 0:
                        pool.wait_ge(rows_done, 1 + t * 2 * TT)
                    else:
                        pool.wait_ge(rows_done, 1 + t * 2 * TT + TT)
                    nc.gpsimd.tensor_tensor(RSTD[:], VE[:], HALF[:], ALU.pow).then_inc(rstd_done, 1)
                rstd(0)
                for g in range(N_G):
                    b = g % 2
                    pool.wait_ge(exp_done, 1 + t * N_S + 4 * (g + 1))
                    pool.sem_inc(pool_on, 1)
                    nc.gpsimd.affine_select(out=P0[:, b, :, 0:J1], in_=P0[:, b, :, 0:J1], pattern=[[0, 4], [1, J1]],
                                            compare_op=ALU.is_ge, fill=0.0, base=AHEAD,
                                            channel_multiplier=-1).then_inc(sel_done, 1)
                    nc.gpsimd.affine_select(out=P1[:, b, :, 0:128], in_=P1[:, b, :, 0:128], pattern=[[0, 4], [1, 128]],
                                            compare_op=ALU.is_ge, fill=0.0, base=J1 + AHEAD - 128,
                                            channel_multiplier=-1).then_inc(sel_done, 1)
                rstd(1)
                for ib in range(IB):
                    pool.wait_ge(in_high, 1 + t * IB + ib + 1)
                    nc.gpsimd.tensor_tensor(IN[:, ib, 1, :], GU[:, ib % 2, :], IN[:, ib, 0, :].bitcast(F32),
                                            ALU.subtract).then_inc(in_low, 1)

        @block.scalar
        def _(act):
            act.wait_ge(raw_loaded, 48)
            nc.scalar.activation(WQKh[:], RAW[:, 0:4 * D].rearrange("p (k n) -> p k n", k=KB), ACT.Copy).then_inc(pre_act, 1)
            for i, w in ((2, WV), (3, WO)):
                nc.scalar.activation(w[:, :, 0:D],
                                     RAW[:, i * KB * D:(i + 1) * KB * D].rearrange("p (k n) -> p k n", k=KB),
                                     ACT.Copy).then_inc(pre_act, 1)
            act.wait_ge(points_loaded, 32)
            act.wait_ge(coef_done, 8)
            for m in range(3):
                for g in range(GI):
                    i = nc.scalar.activation(SW[:, m, g, :], FR[:, g, :], ACT.Identity,
                                             bias=CO[:, m, 1, g:g + 1], scale=CO[:, m, 2, g:g + 1])
                i.then_inc(lin_start, 1)
            for u in range(12):
                act.wait_ge(pre_pe, u + 1)
                nc.scalar.activation(spline_part(u, 0), spline_bank(u), ACT.Copy).then_inc(pre_act, 1)

            with act.Fori(0, TURNS) as t:
                def turn_high_part(dst, u):
                    act.wait_ge(turned, 1 + t * N_TURN + u + 1)
                    nc.scalar.activation(dst, TURN_BANK[:], ACT.Copy).then_inc(turn_high, 1)

                for kb in range(KB):
                    if kb == 0:
                        act.wait_ge(lin_done, 1 + t * N_LIN)
                    turn_high_part(ZT[:, 0, kb, :], T_Z + kb)
                for mb in range(4):
                    act.wait_ge(lin_done, 1 + t * N_LIN + U_QK + mb + 1)
                    if mb == 0:
                        act.wait_ge(qk_stored, 1 + t * 64)
                    else:
                        act.wait_ge(qk_stored, 1 + t * 64 + mb * 16)
                    nc.scalar.activation(QKE[:, 0, :], LIN_BANK[(U_QK + mb) % 4][:], ACT.Copy).then_inc(lin_high, 1)

                def second_half(u, read, n):
                    act.wait_ge(lin_done, 1 + t * N_LIN + u + 1)
                    act.wait_ge(read, 1 + n)
                    nc.scalar.activation(VC[:], LIN_BANK[u % 4][:, D:2 * D], ACT.Copy).then_inc(lin_high, 1)
                for j in range(TT):
                    if j == 0:
                        second_half(U_V, y_done, t * TT)
                    else:
                        second_half(U_V + j, v_done, t * TT + j)
                for g in range(N_G):
                    b = g % 2
                    for q in range(4):
                        u = 4 * g + q
                        n = (S, W1)[q % 2]
                        dst = (P0, P1)[q % 2][:, b, 2 * (q // 2):2 * (q // 2) + 2, :]
                        act.wait_ge(st_done, 1 + t * N_S + u + 1)
                        if q == 0:
                            act.wait_ge(av_done, 1 + t * N_G + max(0, g - 1))
                        nc.scalar.activation(dst, S_BANK[u % 2][:, 0:2 * n].rearrange("p (a i) -> p a i", a=2),
                                             ACT.Exp, scale=SCALE).then_inc(exp_done, 1)
                    if g >= 1:
                        evac_ot(act, t, g - 1)
                evac_ot(act, t, N_G - 1)
                for kb in range(KB):
                    turn_high_part(YT[:, 0, kb, :], T_ON + kb)
                for j in range(TT):
                    if j == 0:
                        second_half(U_WO, v_done, t * TT + TT)
                    else:
                        second_half(U_WO + j, x1_done, t * TT + j)
                for kb in range(KB):
                    if kb == 0:
                        act.wait_ge(lin_done, 1 + t * N_LIN + U_GU)
                    turn_high_part(YT[:, 0, kb, :], T_Z2 + kb)
                for ib in range(IB):
                    u = U_GU + 2 * ib
                    act.wait_ge(lin_done, 1 + t * N_LIN + u + 1)
                    if ib >= 2:
                        act.wait_ge(in_low, 1 + t * IB + ib - 1)
                    else:
                        act.wait_ge(in_low, 1 + t * IB)
                    nc.scalar.activation(GU[:, ib % 2, :], LIN_BANK[u % 4][:], ACT.Tanh, scale=0.5).then_inc(tanh_done, 1)
                    act.wait_ge(up_done, 1 + t * IB + ib + 1)
                    if ib == 0:
                        act.wait_ge(lin_done, 1 + t * N_LIN)
                    nc.scalar.activation(IN[:, ib, 0, :], GU[:, ib % 2, :], ACT.Copy).then_inc(in_high, 1)
                for j in range(TT):
                    if j == 0:
                        second_half(U_DN, x1_done, t * TT + TT)
                    else:
                        second_half(U_DN + j, y_done, t * TT + j)

        @block.vector
        def _(dve):
            dve.wait_ge(points_loaded, 32)
            k = [0]

            def own(i):
                k[0] += 1
                i.then_inc(coef_done, 1)
                dve.wait_ge(coef_done, k[0])
            p0, p1, p2, p3 = (CP[:, :, i, :] for i in range(4))
            a1, a2, a3 = (CO[:, :, i, :] for i in range(3))
            stt = nc.vector.scalar_tensor_tensor
            own(nc.vector.tensor_tensor(a1, p2, p0, ALU.subtract))
            own(stt(out=CT[:], in0=p1, scalar=-5.0, in1=p3, op0=ALU.mult, op1=ALU.subtract))
            own(stt(out=CT[:], in0=p2, scalar=4.0, in1=CT[:], op0=ALU.mult, op1=ALU.add))
            own(stt(out=a2, in0=p0, scalar=2.0, in1=CT[:], op0=ALU.mult, op1=ALU.add))
            own(stt(out=CT[:], in0=p1, scalar=3.0, in1=p0, op0=ALU.mult, op1=ALU.subtract))
            own(stt(out=CT[:], in0=p2, scalar=-3.0, in1=CT[:], op0=ALU.mult, op1=ALU.add))
            own(nc.vector.tensor_tensor(a3, CT[:], p3, ALU.add))
            own(nc.vector.tensor_scalar(CT[:], p1, 0.5, None, ALU.mult))
            dve.wait_ge(pre_act, 3)
            nc.vector.tensor_tensor(WQKl[:], RAW[:, 0:4 * D].rearrange("p (k n) -> p k n", k=KB),
                                    WQKh[:].bitcast(F32), ALU.subtract).then_inc(pre_dve, 1)
            for i, w in ((2, WV), (3, WO)):
                nc.vector.tensor_tensor(w[:, :, D:2 * D],
                                        RAW[:, i * KB * D:(i + 1) * KB * D].rearrange("p (k n) -> p k n", k=KB),
                                        w[:, :, 0:D].bitcast(F32), ALU.subtract).then_inc(pre_dve, 1)
            for m in range(3):
                dve.wait_ge(lin_start, m + 1)
                own(nc.vector.tensor_tensor(SW[:, m], SW[:, m], FR[:], ALU.mult))
                for g in range(GI):
                    i = stt(out=SW[:, m, g, :], in0=SW[:, m, g, :], scalar=CO[:, m, 0, g:g + 1], in1=FR[:, g, :],
                            op0=ALU.add, op1=ALU.mult)
                own(i)
                for g in range(GI):
                    p = CP[:, m, 1, g:g + 1] if m < 2 else CT[:, m, g:g + 1]
                    i = nc.vector.tensor_scalar(SW[:, m, g, :], SW[:, m, g, :], 0.5 if m < 2 else 0.25, p,
                                                ALU.mult, ALU.add)
                i.then_inc(spline_done, 1)
            for u in range(12):
                dve.wait_ge(pre_act, 3 + u + 1)
                nc.vector.tensor_tensor(spline_part(u, 1), spline_bank(u), spline_part(u, 0).bitcast(F32),
                                        ALU.subtract).then_inc(pre_dve, 1)

            with dve.Fori(0, TURNS) as t:
                step = [0]

                def own_step(i):
                    step[0] += 1
                    i.then_inc(dve_step, 1)
                    dve.wait_ge(dve_step, 1 + t * N_STEP + step[0])

                def layer_norm(src, n):
                    for j in range(TT):
                        i = nc.vector.bn_stats(ST[:, j, :], src[:, j, :])
                    own_step(i)
                    dve.sem_inc(dve_on, 1)
                    for j in range(TT):
                        i = nc.vector.bn_aggr(MV[:, j, :], ST[:, j, :])
                    own_step(i)
                    nc.vector.tensor_scalar(VE[:], MV[:, :, 1], EPS, None, ALU.add).then_inc(var_done, 1)
                    dve.wait_ge(rstd_done, 1 + t * 2 + n + 1)
                    for j in range(TT):
                        nc.vector.tensor_scalar(Z[:, j, :], src[:, j, :], MV[:, j, 0:1], RSTD[:, j:j + 1],
                                                ALU.subtract, ALU.mult).then_inc(rows_done, 1)

                def turn_low_part(buf, kb, n, done):
                    dve.wait_ge(turn_high, 1 + t * 3 * KB + n * KB + kb + 1)
                    nc.vector.tensor_tensor(buf[:, 1, kb, :], TURN_BANK[:], buf[:, 0, kb, :].bitcast(F32),
                                            ALU.subtract).then_inc(done, 1)

                dve.wait_ge(x_loaded, 1 + 16 * t + 16)
                dve.wait_ge(turned, 1 + t * N_TURN)
                layer_norm(X, 0)
                for kb in range(KB):
                    turn_low_part(ZT, kb, 0, z_low)
                for mb in range(4):
                    dve.wait_ge(lin_high, 1 + t * N_HIGH + mb + 1)
                    nc.vector.tensor_tensor(QKE[:, 1, :], LIN_BANK[(U_QK + mb) % 4][:], QKE[:, 0, :].bitcast(F32),
                                            ALU.subtract).then_inc(qk_split, 1)
                for j in range(TT):
                    u = U_V + j
                    dve.wait_ge(lin_high, 1 + t * N_HIGH + 4 + j + 1)
                    if j == 0:
                        dve.wait_ge(av_done, 1 + t * N_G)
                    nc.vector.tensor_tensor(V[:, j, :, 0, :], LIN_BANK[u % 4][:, 0:D].rearrange("p (h c) -> p h c", c=DH),
                                            VC[:].rearrange("p (h c) -> p h c", c=DH), ALU.add).then_inc(v_done, 1)
                dve.wait_ge(turned, 1 + t * N_TURN)
                for u in range(N_S):
                    s, p, it = u // (2 * NP), u // 2 % NP, u % 2
                    n = (128 + AHEAD, S)[it]
                    dve.wait_ge(s1_done, 1 + t * N_S + u + 1)
                    nc.vector.tensor_reduce(out=M[:, s, it, :].rearrange("p (a k) -> p a k", a=2)[:, :, p],
                                            in_=S_BANK[u % 2][:, 0:2 * n].rearrange("p (a j) -> p a j", a=2),
                                            axis=AX.X, op=ALU.max, negate=True).then_inc(max_done, 1)
                dve.wait_ge(m_loaded, 1 + 32 * t)
                for s in range(SEQS):
                    dve.wait_ge(turned, 1 + t * N_TURN + T_M + s + 1)
                    nc.vector.tensor_copy(MT[:, s * S:(s + 1) * S], TURN_BANK[0:H, 0:S]).then_inc(mt_done, 1)
                for j in range(TT):
                    dve.wait_ge(turned, 1 + t * N_TURN + T_O + j + 1)
                    heads = TURN_BANK[:].rearrange("p (h c) -> p h c", c=2 * DH)
                    own_step(nc.vector.reciprocal(R[:], heads[:, :, DH]))
                    nc.vector.tensor_tensor(Z[:, j, :].rearrange("p (h c) -> p h c", c=DH), heads[:, :, 0:DH],
                                            R[:].unsqueeze(2).broadcast_to([128, H, DH]), ALU.mult).then_inc(o_done, 1)
                for kb in range(KB):
                    turn_low_part(YT, kb, 1, on_low)

                def residual(dst, src, u, high, done):
                    dve.wait_ge(lin_high, 1 + t * N_HIGH + high + 1)
                    own_step(nc.vector.tensor_tensor(dst, src, VC[:], ALU.add))
                    nc.vector.tensor_tensor(dst, dst, LIN_BANK[u % 4][:, 0:D], ALU.add).then_inc(done, 1)
                dve.wait_ge(y_stored, 1 + 16 * t)
                for j in range(TT):
                    residual(X1[:, j, :], X[:, j, :], U_WO + j, 8 + j, x1_done)
                dve.wait_ge(x1_done, 1 + t * TT + TT)
                layer_norm(X1, 1)
                for kb in range(KB):
                    turn_low_part(YT, kb, 2, z2_low)
                for ib in range(IB):
                    u = U_GU + 2 * ib
                    g = GU[:, ib % 2, :]
                    dve.wait_ge(tanh_done, 1 + t * IB + ib + 1)
                    own_step(stt(out=g, in0=g, scalar=1.0, in1=LIN_BANK[u % 4][:], op0=ALU.add, op1=ALU.mult))
                    dve.wait_ge(lin_done, 1 + t * N_LIN + u + 2)
                    nc.vector.tensor_tensor(g, g, LIN_BANK[(u + 1) % 4][:], ALU.mult).then_inc(up_done, 1)
                for j in range(TT):
                    residual(X1[:, j, :], X1[:, j, :], U_DN + j, 12 + j, y_done)
                assert step[0] == N_STEP

        @block.tensor
        def _(pe):
            mm = nc.tensor.matmul
            pe.wait_ge(const_loaded, 48)
            pe.wait_ge(wn_loaded, 48)
            for u in range(12):
                if u >= 4:
                    pe.wait_ge(pre_dve, 3 + u - 3)
                for q in range(4):
                    if u < 8:
                        m, kb, ob = u // 4, u // 2 % 2, u % 2 * 4 + q
                        src = WN[:, m, ob * D + kb * 128:ob * D + kb * 128 + 128]
                        dst = LIN_BANK[u % 4][:, q * 128:(q + 1) * 128]
                    else:
                        ib, hb = 2 * (u - 8) + q // 2, q % 2
                        src = WN[:, 2, hb * INTER + ib * 128:hb * INTER + ib * 128 + 128]
                        dst = LIN_BANK[u % 4][:, q * 128:(q + 1) * 128]
                    i = nc.tensor.transpose(dst, src, ID[:])
                i.then_inc(pre_pe, 1)
            pe.wait_ge(pre_dve, 3 + 12)

            with pe.Fori(0, TURNS) as t:
                def turn_rows(kb):
                    for j in range(TT):
                        i = nc.tensor.transpose(TURN_BANK[:, j * 128:(j + 1) * 128],
                                                Z[:, j, kb * 128:(kb + 1) * 128], ID[:])
                    i.then_inc(turned, 1)

                def columns(u, wh, wl, act):
                    b = LIN_BANK[u % 4]
                    for kb in range(KB):
                        mm(b[:], wh[:, kb], act[:, 0, kb, :], start=kb == 0, stop=False)
                        mm(b[:], wh[:, kb], act[:, 1, kb, :], start=False, stop=False)
                        i = mm(b[:], wl[:, kb], act[:, 0, kb, :], start=False, stop=kb == KB - 1)
                    i.then_inc(lin_done, 1)

                def rows(u, blocks, act, w):
                    b = LIN_BANK[u % 4]
                    for k in range(blocks):
                        if k < blocks - 1:
                            mm(b[:], act(k, 0), w[:, k, :], start=k == 0, stop=False, skip_group_check=True)
                        mm(b[:, 0:D], act(k, 1), w[:, k, 0:D], start=False, stop=False, skip_group_check=True)
                    mm(b[:], act(k, 0), w[:, k, :], start=False, stop=True,
                       skip_group_check=True).then_inc(lin_done, 1)

                pe.wait_ge(rows_done, 1 + t * 2 * TT + TT)
                pe.wait_ge(z2_low, 1 + t * KB)
                turn_rows(0)
                pe.wait_ge(z_low, 1 + t * KB + 1)
                turn_rows(1)
                pe.wait_ge(z_low, 1 + t * KB + 2)
                pe.wait_ge(y_done, 1 + t * TT)
                for mb in range(4):
                    c = slice(mb * 128, (mb + 1) * 128)
                    columns(U_QK + mb, WQKh[:, :, c], WQKl[:, :, c], ZT)
                for j in range(TT):
                    pe.wait_ge(qk_split, 1 + t * 4 + j + 1)
                    rows(U_V + j, KB, lambda k, part: ZT[:, part, k, j * 128:(j + 1) * 128], WV)
                pe.wait_ge(pre_pool, 3)
                pe.wait_ge(ks_loaded, 1 + t * 96 + 96)
                pe.wait_ge(qm_loaded, 1 + t * 96 + 96)
                pe.wait_ge(zero_loaded, 1 + t * 32 + 32)
                for u in range(N_S):
                    s, p, it = u // (2 * NP), u // 2 % NP, u % 2
                    n = (128 + AHEAD, S)[it]
                    b = S_BANK[u % 2]
                    if u < 2:
                        pe.wait_ge(exp_done, 1 + t * N_S)
                    else:
                        pe.wait_ge(max_done, 1 + t * N_S + u - 1)
                    i0 = s * S + it * 128
                    for a in range(2):
                        mm(b[:, a * n:(a + 1) * n], QM[:, p, a, i0:i0 + 128], KS[:, p, s * S:s * S + n],
                           start=a == 0, stop=False, skip_group_check=True)
                    c0 = AHEAD + it * 128
                    w = n - c0
                    mm(b[:, 0:2 * n].rearrange("p (a j) -> p a j", a=2)[:, :, c0:n], IDB[:],
                       UP[:, 0:w].unsqueeze(1).broadcast_to([128, 2, w]), start=False, stop=True,
                       skip_group_check=True).then_inc(s1_done, 1)
                for s in range(SEQS):
                    pe.wait_ge(max_done, 1 + t * N_S + (s + 1) * 2 * NP)
                    if s == 0:
                        pe.wait_ge(z_low, 1 + t * KB + KB)
                    else:
                        pe.wait_ge(mt_done, 1 + t * SEQS + s)
                    for it in range(2):
                        i = nc.tensor.transpose(TURN_BANK[0:H, it * 128:(it + 1) * 128], M[:, s, it, :], ID[:])
                    i.then_inc(turned, 1)

                def scores(g):
                    s = g // NG
                    for q in range(4):
                        u = 4 * g + q
                        p, jt = 2 * (g % NG) + q // 2, q % 2
                        n = (S, W1)[jt]
                        if u >= 2:
                            pe.wait_ge(exp_done, 1 + t * N_S + u - 1)
                        mm(S_BANK[u % 2][:, 0:2 * n], KS[:, p, s * S + jt * 128:s * S + jt * 128 + 128],
                           QM[:, p, :, s * S + (S - n):s * S + S], start=True, stop=True).then_inc(st_done, 1)

                def weigh(g):
                    pe.wait_ge(sel_done, 1 + t * 2 * N_G + 2 * g + 2)
                    pe.wait_ge(ot_done, 1 + t * N_G + g)
                    for jt in range(2):
                        for hl in range(4):
                            n = (S, W1)[jt]
                            i = mm(AV_BANK[32 * hl:32 * hl + 32, S - n:S],
                                   values(g // NG * 2 + jt, g % NG * 4 + hl),
                                   (P0, P1)[jt][:, g % 2, hl, :], start=jt == 0, stop=jt == 1)
                    i.then_inc(av_done, 1)

                pe.wait_ge(m_loaded, 1 + t * 32 + 32)
                pe.wait_ge(v_done, 1 + t * TT + TT)
                scores(0)
                for g in range(N_G):
                    if g + 1 < N_G:
                        scores(g + 1)
                    weigh(g)
                    if g % NG == NG - 1:
                        pe.wait_ge(ot_done, 1 + t * N_G + g + 1)
                        for it in range(2):
                            j = g // NG * 2 + it
                            if j == 0:
                                pe.wait_ge(mt_done, 1 + t * SEQS + SEQS)
                            else:
                                pe.wait_ge(o_done, 1 + t * TT + j)
                            for c in range(NG):
                                i = nc.tensor.transpose(TURN_BANK[:, c * 128:(c + 1) * 128],
                                                        OT[:, c, it * 128:(it + 1) * 128], ID[:])
                            i.then_inc(turned, 1)
                pe.wait_ge(o_done, 1 + t * TT + TT)
                turn_rows(0)
                pe.wait_ge(on_low, 1 + t * KB + 1)
                turn_rows(1)
                pe.wait_ge(on_low, 1 + t * KB + 2)
                for j in range(TT):
                    rows(U_WO + j, KB, lambda k, part: YT[:, part, k, j * 128:(j + 1) * 128], WO)
                pe.wait_ge(rows_done, 1 + t * 2 * TT + 2 * TT)
                turn_rows(0)
                pe.wait_ge(z2_low, 1 + t * KB + 1)
                turn_rows(1)
                pe.wait_ge(z2_low, 1 + t * KB + 2)
                for ib in range(IB):
                    if ib < 2:
                        pe.wait_ge(x1_done, 1 + t * TT + TT)
                    else:
                        pe.wait_ge(up_done, 1 + t * IB + ib - 1)
                    for m in range(2):
                        c = slice(ib * 128, (ib + 1) * 128)
                        columns(U_GU + 2 * ib + m, WGUh[:, m, :, c], WGUl[:, m, :, c], YT)
                pe.wait_ge(in_low, 1 + t * IB + IB)
                for j in range(TT):
                    pe.wait_ge(up_done, 1 + t * IB + IB)
                    rows(U_DN + j, IB, lambda k, part: IN[:, k, part, j * 128:(j + 1) * 128], WD)


def kernel(L0_attn_x, L0_attn_wq, L0_attn_wk, L0_attn_wv, L0_attn_wo, L0_ffn_gate_cp, L0_ffn_up_cp,
           L0_ffn_down_cp):
    import ml_dtypes
    import concourse.bacc as bacc
    from concourse.bass_utils import run_bass_kernel_spmd

    def windows(cp):
        cp = np.asarray(cp)
        at = np.clip(np.arange(GI * 128)[None, :] + np.arange(-1, 3)[:, None], 0, NC - 1)
        return cp[at].reshape(4, GI, 128)

    points = np.stack([windows(c) for c in (L0_ffn_gate_cp, L0_ffn_up_cp, L0_ffn_down_cp)])
    arrays = {
        "x": np.asarray(L0_attn_x).reshape(B * S, D),
        "wqk": np.concatenate([np.asarray(L0_attn_wq).T, np.asarray(L0_attn_wk).T], axis=1),
        "wv": np.asarray(L0_attn_wv).T,
        "wo": np.asarray(L0_attn_wo).T,
        "points": points.transpose(3, 0, 1, 2).reshape(128, -1),
        "fractions": fraction_table(),
        "ident": np.eye(128, dtype=np.float32),
        "identb": np.eye(128, dtype=ml_dtypes.bfloat16),
        "upper": (np.triu(np.ones((128, 128)), 1) * NEG).astype(ml_dtypes.bfloat16),
    }
    arrays = {k: np.ascontiguousarray(v) for k, v in arrays.items()}
    nc = bacc.Bacc("TRN2", target_bir_lowering=False, num_devices=1)
    args = [nc.dram_tensor(k, v.shape, mybir.dt.from_np(v.dtype), kind="ExternalInput").ap()
            for k, v in arrays.items()]
    out = nc.dram_tensor("out", (B * S, D), F32, kind="ExternalOutput").ap()
    build(nc, *args, out)
    r = run_bass_kernel_spmd(nc, [arrays], core_ids=[0])
    return r.results[0]["out"].reshape(B, S, D)
```

```python
from contextlib import ExitStack

import numpy as np

import concourse.bass as bass
from concourse import mybir

F32 = mybir.dt.float32
F32R = mybir.dt.float32r
BF16 = mybir.dt.bfloat16
ALU = mybir.AluOpType
ACT = mybir.ActivationFunctionType
AX = mybir.AxisListType

B, S, D = 16, 256, 256
H, DH = 16, 16
INTER = 1024
WINDOW = 32
AHEAD = WINDOW // 2
EPS = 1e-5
SCALE = DH ** -0.5
NEG = -1e30

SEQS = 2
T = SEQS * S
TURNS = B // SEQS
TT = T // 128
KB = D // 128
IB = INTER // 128
NP = H // 2
NG = H // 4
J1 = 128 - AHEAD
W1 = S - J1
STACK = 64
MROW = 3 * DH

COMPRESSION = 128.9
NW = INTER * D
NC = max(16, int(NW / COMPRESSION))
NI = NC - 1


def spline_grid():
    t = np.linspace(0.0, NC - 1.0, NW, dtype=np.float64)
    i = np.clip(np.floor(t).astype(np.int64), 0, NC - 2)
    f = (t - i).astype(np.float32)
    first = np.searchsorted(i, np.arange(NI))
    return i, f, first, np.append(first[1:], NW) - first


GRID_I, GRID_F, FIRST, COUNT = spline_grid()
LEN = int(COUNT.min())
GI = -(-NI // 128)
assert COUNT.max() == LEN + 1


def fraction_table():
    table = np.zeros((GI * 128, LEN + 1), np.float32)
    for i in range(NI):
        table[i, :COUNT[i]] = GRID_F[FIRST[i]:FIRST[i] + COUNT[i]]
    return np.ascontiguousarray(table.reshape(GI, 128, LEN + 1).transpose(1, 0, 2)).reshape(128, -1)


def spline_runs():
    runs, i = [], 0
    while i < NI:
        n = 1
        while i + n < NI and (i + n) % 128 and FIRST[i + n] - FIRST[i] == LEN * n:
            n += 1
        runs.append((i, n))
        i += n
    return runs


N_S = SEQS * NP * 2
N_G = SEQS * NG
FRONT = ([("ln1a", 0), ("ln1b", 0), ("ln1a", 1), ("ln1b", 1), ("zt", 0), ("zt", 1)]
         + [("qk", m) for m in range(4)] + [("load", 0)] + [("v", j) for j in range(TT)])


GU_BEFORE = 12
LATE = [("wo", 2), ("wo", 3), ("ln2a", 1), ("ln2b", 1), ("z2", 1)]


def order(back, front, early=()):
    early = dict(early)
    steps = [("x", 0)] if front else []
    gu = 0
    for k in range(N_S // 2):
        steps += [("s1", 2 * k), ("s1", 2 * k + 1)]
        if back:
            steps += {0: LATE[0:2], 2: LATE[2:3], 4: LATE[3:4], 5: LATE[4:5]}.get(k, [])
        if back and k >= 6:
            steps += [("gu", gu)]
            gu += 1
        if k == N_S // 4:
            steps += [("mt", 0)]
        if front:
            steps += {7: [("ln1a", 0)], 9: [("ln1a", 1)], 11: [("ln1b", 0)], 13: [("ln1b", 1)]}.get(k, [])
        steps += early.get(("s1", k), [])
    steps += [("mt", 1)]
    if back:
        steps += [("gu", gu)]
    if front:
        steps += [("zt", 0)]
    if back:
        steps += [("gu", n) for n in range(gu + 1, GU_BEFORE)]
    if front:
        steps += [("zt", 1)] + [("qk", m) for m in range(4)]
    steps += [("sc", 0)]
    for g in range(N_G):
        if g + 1 < N_G:
            steps += [("sc", g + 1)]
        elif front:
            steps += [("load", 0)]
        if g == NG:
            steps += [("ot", 0), ("ot", 1)]
        steps += [("av", g)]
        if g == NG + 1:
            steps += [("on", 0)]
        if back:
            steps += [("gu", GU_BEFORE + g)] if g < NG else [("dn", g - NG)]
        if g == NG + 2:
            steps += [("xr", 0)]
        steps += early.get(("av", g), [])
    steps += [("xr", 1), ("ot", 2), ("wo", 0), ("wo", 1), ("ot", 3)]
    v = [("v", j) for j in range(TT)] if front else []
    steps += v[0:1] + [("ln2a", 0)] + v[1:2] + [("on", 1)] + v[2:4] + [("ln2b", 0), ("z2", 0)]
    return steps + early.get("end", [])


BACK_ONLY = LATE + [("gu", n) for n in range(2 * IB)] + [("dn", j) for j in range(TT)]


def at(turn, each, n):
    t, off = turn
    return t * each + (off * each + n + 1)


def build(nc, x, wqk, wv, wo, points, fractions, ident, identb, upper, out):
    ctx = ExitStack()
    with ctx:
        def sb(name, shape, dt=F32):
            return ctx.enter_context(nc.sbuf_tensor(name, shape, dt))

        def sem(name):
            return ctx.enter_context(nc.semaphore(name))

        qk_scratch = nc.dram_tensor("qk_scratch", (2, 2, 2, DH, NP, T), F32, kind="Internal").ap()
        w_scratch = nc.dram_tensor("w_scratch", (3, NW), F32, kind="Internal").ap()

        ID = sb("ID", [128, 128])
        IDB = sb("IDB", [128, 128], BF16)
        UP = sb("UP", [128, 128], BF16)
        WQKh = sb("WQKh", [128, KB, 2 * D], F32R)
        WQKl = sb("WQKl", [128, KB, 2 * D], F32R)
        WV = sb("WV", [128, KB, 2 * D], F32R)
        WO = sb("WO", [128, KB, 2 * D], F32R)
        WGUh = sb("WGUh", [128, 2, KB, INTER], F32R)
        WGUl = sb("WGUl", [128, 2, KB, INTER], F32R)
        WD = sb("WD", [128, IB, 2 * D], F32R)
        X = sb("X", [128, TT, D])
        X1 = sb("X1", [128, TT, D])
        Z = sb("Z", [128, TT, D])
        ST, MV, VE, RSTD = ([sb(f"{n}{i}", [128, TT] + w) for i in range(2)]
                            for n, w in (("ST", [6]), ("MV", [2]), ("VE", []), ("RSTD", [])))
        HALF = sb("HALF", [128, SEQS])
        ZT = sb("ZT", [128, 2, KB, T], F32R)
        YT = sb("YT", [128, 2, KB, T], F32R)
        QKE = sb("QKE", [128, 2, T], F32R)
        QM = sb("QM", [128, NP, 2, T], F32R)
        KS = sb("KS", [128, NP, T], F32R)
        V = sb("V", [128, TT, H, 2, DH])
        M = sb("M", [128, SEQS, 2, H])
        P0 = sb("P0", [128, 2, 4, S])
        P1 = sb("P1", [128, 2, 4, W1])
        OT = sb("OT", [128, NG, S])
        MT = OT[0:H, 2:4, :]
        R = sb("R", [128, H])
        VC = sb("VC", [128, D])
        QK_OUT = [P0[:, i, :, :].rearrange("p h i -> p (h i)").rearrange("p (a t) -> p a t", a=2).bitcast(F32R)
                  for i in range(2)]
        QK_OUT += [QKE[:], Z[:, :, :].rearrange("p j d -> p (j d)").rearrange("p (a t) -> p a t", a=2).bitcast(F32R)]

        with ExitStack() as early:
            FR = early.enter_context(nc.sbuf_tensor("FR", [128, GI, LEN + 1], F32))
            SW = early.enter_context(nc.sbuf_tensor("SW", [128, 3, GI, LEN + 1], F32))
            CP = early.enter_context(nc.sbuf_tensor("CP", [128, 3, 4, GI], F32))
            CO = early.enter_context(nc.sbuf_tensor("CO", [128, 3, 3, GI], F32))
            CT = early.enter_context(nc.sbuf_tensor("CT", [128, 3, GI], F32))
        WN = SW[:, :, :, :].rearrange("p m g s -> p (m g s)")[:, 0:3 * 2 * INTER].rearrange(
            "p (m c) -> p m c", m=3)
        GU = sb("GU", [128, 2, T])
        IN = sb("IN", [128, IB, 2, T], F32R)
        RAW = P0[:, :, :, :].rearrange("p a b c -> p (a b c)")

        bank = [ctx.enter_context(nc.psum_tensor(f"bank{i}", [128, 512], F32)) for i in range(8)]
        S_BANK = bank[0:2]
        AV_BANK = bank[2]
        TURN_BANK = bank[3]
        LIN_BANK = bank[4:8]
        TURN_KT = TURN_BANK[:].rearrange("p (k t) -> p k t", k=KB)

        const_loaded, raw_loaded, points_loaded, w_stored, wn_loaded = map(sem, (
            "const_loaded", "raw_loaded", "points_loaded", "w_stored", "wn_loaded"))
        x_loaded, qm_loaded, ks_loaded, zero_loaded = map(sem, (
            "x_loaded", "qm_loaded", "ks_loaded", "zero_loaded"))
        xr_loaded, m_loaded, y_stored = ([sem(f"{n}{s}") for s in range(SEQS)]
                                         for n in ("xr_loaded", "m_loaded", "y_stored"))
        qk_stored = [sem(f"qk_stored{n}") for n in range(4)]
        filled, raw_high, raw_low, coef_done, affine_done, cubic_done, spline_done, wt_done, wt_high, wt_low = map(
            sem, ("filled", "raw_high", "raw_low", "coef_done", "affine_done", "cubic_done", "spline_done",
                  "wt_done", "wt_high", "wt_low"))
        z_turned, qk_done, v_prod, s1_done, mt_turned, st_done, av_done, o_turned, on_turned, wo_prod = map(sem, (
            "z_turned", "qk_done", "v_prod", "s1_done", "mt_turned", "st_done", "av_done", "o_turned",
            "on_turned", "wo_prod"))
        z2_turned, gu_prod, dn_prod = map(sem, ("z2_turned", "gu_prod", "dn_prod"))
        z_high, qk_high, v_half, exp_done, ot_done, on_high, z2_high, tanh_done, in_high = map(
            sem, ("z_high", "qk_high", "v_half", "exp_done", "ot_done", "on_high", "z2_high",
                  "tanh_done", "in_high"))
        step_done, z_low, qk_split, v_done, max_done, mt_done, o_done, on_low, x1_done, z2_low = map(sem, (
            "step_done", "z_low", "qk_split", "v_done", "max_done", "mt_done", "o_done", "on_low", "x1_done",
            "z2_low"))
        gate_done, up_done, y_done, bn_on = map(sem, ("gate_done", "up_done", "y_done", "bn_on"))
        var_done, rstd_done, rows_done = ([sem(f"{n}{i}") for i in range(2)] for n in ("var", "rstd", "rows"))
        sel_done, in_low, pool_on = map(sem, ("sel_done", "in_low", "pool_on"))

        loop_sems = [x_loaded, qm_loaded, ks_loaded, zero_loaded,
                     z_turned, qk_done, v_prod, s1_done, mt_turned, st_done, av_done, o_turned, on_turned,
                     wo_prod, z2_turned, gu_prod, dn_prod, z_high, qk_high, v_half, exp_done, ot_done, on_high,
                     z2_high, tanh_done, in_high, step_done, z_low, qk_split, v_done,
                     max_done, mt_done, o_done, on_low, x1_done, z2_low, gate_done, up_done, y_done, sel_done,
                     in_low] + var_done + rstd_done + rows_done + xr_loaded + m_loaded + y_stored + qk_stored

        DMA = 16
        N_QS, N_QM, N_ZERO, N_M = 2 * DMA, 4 * DMA, 2 * DMA, 2 * DMA

        runs = spline_runs()
        extra = [int(i) for i in np.nonzero(COUNT == LEN + 1)[0]]
        W_PIECES = [(i, n, 0, LEN) for i, n in runs] + [(i, 1, LEN, 1) for i in extra]
        W_CHUNK = 6
        N_CHUNKS = -(-len(W_PIECES) // W_CHUNK)

        stores = [("ws", i) for i in range(N_CHUNKS)]
        EARLY = {("s1", 4): [("sd", 2), ("sb", 2)],
                 ("s1", 8): stores[0:2], ("s1", 12): stores[2:4],
                 ("av", 0): stores[4:5], ("av", 1): stores[5:6], ("av", 2): stores[6:7],
                 ("av", 3): stores[7:] + [("wl", 0)],
                 "end": [("wt", u) for u in range(12)]}
        STARTUP = ([("raw", 0)] + FRONT
                   + [("co", 0), ("sa", 0), ("sa", 1), ("sa", 2), ("sd", 0), ("sb", 0), ("sd", 1), ("sb", 1)])
        FIRST_TURN = order(False, True, EARLY)
        MIDDLE_TURN = order(True, True)
        LAST_TURN = order(True, False)

        def values(tile, h):
            return V[:, tile, h, :, :].rearrange("p a c -> p (a c)")

        def spline_bank(u):
            b = LIN_BANK[u % 4][:, :]
            return b if u < 8 else b.rearrange("p (a n) -> p a n", a=2)

        def spline_part(u, part):
            if u < 8:
                m, kb, half = u // 4, u // 2 % 2, u % 2
                return (WGUh, WGUl)[part][:, m, kb, half * 512:(half + 1) * 512]
            ib = 2 * (u - 8)
            return WD[:, ib:ib + 2, part * D:(part + 1) * D]

        def seq(buf, part, s):
            return buf[:, part, :, s * S:(s + 1) * S]

        def raw(i, n):
            return RAW[:, i * KB * D:(i + n) * KB * D].rearrange("p (k c) -> p k c", k=KB)

        def run(eng, turn):
            turn(STARTUP, None, None, (0, 0))
            turn(FIRST_TURN, None, (0, 0), (0, 1))
            with eng.Fori(1, TURNS - 1) as t:
                turn(MIDDLE_TURN, (t, -1), (t, 0), (t, 1))
            turn(LAST_TURN, (TURNS - 2, 0), (TURNS - 1, 0), None)
            turn(BACK_ONLY, (TURNS - 1, 0), None, None)

        block = ctx.enter_context(nc.Block())


        @block.sync
        def _(sp):
            def rows_of(dram, turn, s=None):
                t, off = turn
                first, n = (0, T) if s is None else (s * S, S)
                if isinstance(t, int):
                    a = (t + off) * T + first
                    v = dram[a:a + n, :]
                else:
                    v = dram[bass.ds(t * T + (off * T + first), n), :]
                return v.rearrange("(j p) d -> p j d", p=128)

            def turn(steps, b, m, f):
                for what, n in steps:
                    c = b if (what, n) in LATE else m
                    if what == "raw":
                        sp.dma_start(X[:], rows_of(x, (0, 0))).then_inc(x_loaded, DMA)
                        for dst, src in ((ID, ident), (IDB, identb), (UP, upper)):
                            sp.dma_start(dst[:], src).then_inc(const_loaded, DMA)
                        for i, k, w in ((0, 2, wqk), (2, 1, wv), (3, 1, wo)):
                            sp.dma_start(raw(i, k), w.rearrange("(k p) c -> p k c", p=128)).then_inc(raw_loaded, DMA)
                        sp.dma_start(CP[:], points.rearrange("p (m k g) -> p m k g", m=3, k=4)).then_inc(points_loaded, DMA)
                        sp.dma_start(FR[:], fractions.rearrange("p (g s) -> p g s", g=GI)).then_inc(points_loaded, DMA)
                    elif what == "x":
                        sp.wait_ge(rows_done[0], at(f, TT, 0))
                        sp.dma_start(X[:], rows_of(x, f)).then_inc(x_loaded, DMA)
                    elif what == "mt":
                        sp.wait_ge(mt_done, at(m, SEQS, n + 1))
                        for a in range(2):
                            r = STACK * a + MROW
                            sp.dma_start(QM[r:r + 1, :, a, n * S:(n + 1) * S].bitcast(F32),
                                         MT[a * NP:(a + 1) * NP, n, :]).then_inc(m_loaded[n], DMA)
                    elif what == "qk":
                        sp.wait_ge(qk_split, at(f, 4, n + 1))
                        w, half = divmod(n, 2)
                        for part in range(2):
                            sp.dma_start(qk_scratch[w, part, :, :, half * 4:half * 4 + 4, :].rearrange("a d p t -> p (a d) t"),
                                         QK_OUT[n][:, part, :].bitcast(F32)).then_inc(qk_stored[n], DMA)
                    elif what == "load":
                        if m is not None:
                            sp.wait_ge(st_done, at(m, N_S, N_S))
                        else:
                            sp.wait_ge(filled, 3)
                        for a in range(2):
                            r, z = STACK * a + MROW, STACK * (1 - a)
                            sp.dma_start(QM[r:r + 1, :, a, :].bitcast(F32),
                                         QM[z:z + 1, :, a, :].bitcast(F32)).then_inc(zero_loaded, DMA)
                        for i in range(4):
                            sp.wait_ge(qk_stored[i], at(f, N_QS, N_QS))
                        for a in range(2):
                            r = STACK * a
                            q, k = qk_scratch[0, :, a], qk_scratch[1, :, a]
                            sp.dma_start(QM[r:r + 2 * DH, :, a, :].bitcast(F32), q).then_inc(qm_loaded, DMA)
                            sp.dma_start(QM[r + 2 * DH:r + 3 * DH, :, a, :].bitcast(F32), q[0]).then_inc(qm_loaded, DMA)
                            sp.dma_start(KS[r:r + DH, :, :].bitcast(F32), k[0]).then_inc(ks_loaded, DMA)
                            sp.dma_start(KS[r + DH:r + 3 * DH, :, :].bitcast(F32), k).then_inc(ks_loaded, DMA)
                    elif what == "dn" and n % 2:
                        s = n // 2
                        sp.wait_ge(y_done, at(b, TT, n + 1))
                        sp.dma_start(rows_of(out, b, s), X1[:, 2 * s:2 * s + 2, :]).then_inc(y_stored[s], DMA)
                    elif what == "xr":
                        if b is not None:
                            sp.wait_ge(y_stored[n], at(b, DMA, DMA))
                        sp.dma_start(X1[:, 2 * n:2 * n + 2, :], rows_of(x, m, n)).then_inc(xr_loaded[n], DMA)
                    elif what == "ws":
                        if n == 0:
                            sp.wait_ge(spline_done, 3)
                        for i, k, a, w in W_PIECES[n * W_CHUNK:(n + 1) * W_CHUNK]:
                            g, p = divmod(i, 128)
                            c = int(FIRST[i]) + a
                            sp.dma_start(w_scratch[:, c:c + k * w].rearrange("m (p s) -> p m s", s=w),
                                         SW[p:p + k, :, g, a:a + w], allow_slow_non_contiguous=w == 1).then_inc(w_stored, DMA)
                    elif what == "wl":
                        sp.wait_ge(w_stored, DMA * len(W_PIECES))
                        for i, w in enumerate((D, D, INTER)):
                            sp.dma_start(WN[:, i, :].rearrange("p (o c) -> p o c", c=w),
                                         w_scratch[i, :].rearrange("(o p c) -> p o c", p=128, c=w)).then_inc(wn_loaded, DMA)
            for i in loop_sems:
                sp.sem_inc(i, 1)
            run(sp, turn)
            for s in range(SEQS):
                sp.wait_ge(y_stored[s], 1 + DMA * TURNS)

        @block.gpsimd
        def _(pool):
            nc.gpsimd.memset(HALF[:], -0.5).then_inc(filled, 1)
            nc.gpsimd.memset(QM[:].bitcast(F32), 0.0).then_inc(filled, 1)
            pool.wait_ge(filled, 2)
            nc.gpsimd.memset(KS[32:64, :, :].bitcast(F32), 1.0).then_inc(filled, 1)
            pool.wait_ge(filled, 3)
            nc.gpsimd.memset(KS[96:128, :, :].bitcast(F32), 1.0).then_inc(filled, 1)
            pool.wait_ge(filled, 4)
            nc.gpsimd.memset(V[:, :, :, 1, :], 1.0).then_inc(filled, 1)

            def turn(steps, b, m, f):
                for what, n in steps:
                    c = b if (what, n) in LATE else m
                    if what in ("ln1a", "ln2a"):
                        i, own = (0, f) if what == "ln1a" else (1, c)
                        j = slice(2 * n, 2 * n + 2)
                        pool.wait_ge(var_done[i], at(own, SEQS, n + 1))
                        nc.gpsimd.tensor_tensor(RSTD[i][:, j], VE[i][:, j], HALF[:], ALU.pow).then_inc(rstd_done[i], 1)
                    elif what == "sc":
                        k = n % 2
                        pool.wait_ge(exp_done, at(m, N_S, 4 * (n + 1)))
                        pool.sem_inc(pool_on, 1)
                        nc.gpsimd.affine_select(out=P0[:, k, :, 0:J1], in_=P0[:, k, :, 0:J1], pattern=[[0, 4], [1, J1]],
                                                compare_op=ALU.is_ge, fill=0.0, base=AHEAD,
                                                channel_multiplier=-1).then_inc(sel_done, 1)
                        nc.gpsimd.affine_select(out=P1[:, k, :, 0:128], in_=P1[:, k, :, 0:128], pattern=[[0, 4], [1, 128]],
                                                compare_op=ALU.is_ge, fill=0.0, base=J1 + AHEAD - 128,
                                                channel_multiplier=-1).then_inc(sel_done, 1)
                    elif what == "gu" and n % 2:
                        ib = n // 2
                        pool.wait_ge(in_high, at(b, IB, ib + 1))
                        nc.gpsimd.tensor_tensor(IN[:, ib, 1, :], GU[:, ib % 2, :], IN[:, ib, 0, :].bitcast(F32),
                                                ALU.subtract).then_inc(in_low, 1)
            run(pool, turn)

        @block.scalar
        def _(act):
            copy = lambda dst, src: nc.scalar.activation(dst, src, ACT.Copy)

            def turn(steps, b, m, f):
                for what, n in steps:
                    c = b if (what, n) in LATE else m
                    if what == "raw":
                        act.wait_ge(raw_loaded, 3 * DMA)
                        copy(WQKh[:], raw(0, 2)).then_inc(raw_high, 1)
                        copy(WV[:, :, 0:D], raw(2, 1)).then_inc(raw_high, 1)
                        copy(WO[:, :, 0:D], raw(3, 1)).then_inc(raw_high, 1)
                    elif what == "sa":
                        if n == 0:
                            act.wait_ge(points_loaded, 2 * DMA)
                            act.wait_ge(coef_done, 8)
                        for g in range(GI):
                            i = nc.scalar.activation(SW[:, n, g, :], FR[:, g, :], ACT.Identity,
                                                     bias=CO[:, n, 1, g:g + 1], scale=CO[:, n, 2, g:g + 1])
                        i.then_inc(affine_done, 1)
                    elif what == "sb":
                        act.wait_ge(cubic_done, 2 * n + 2)
                        for g in range(GI):
                            p = CP[:, n, 1, g:g + 1] if n < 2 else CT[:, n, g:g + 1]
                            i = nc.scalar.activation(SW[:, n, g, :], SW[:, n, g, :], ACT.Identity, bias=p,
                                                     scale=0.5 if n < 2 else 0.25)
                        i.then_inc(spline_done, 1)
                    elif what == "wt":
                        act.wait_ge(wt_done, n + 1)
                        copy(spline_part(n, 0), spline_bank(n)).then_inc(wt_high, 1)
                    elif what == "zt":
                        act.wait_ge(z_turned, at(f, SEQS, n + 1))
                        if n == 0:
                            act.wait_ge(v_prod, at(f, TT, 0))
                        copy(seq(ZT, 0, n), TURN_KT).then_inc(z_high, 1)
                    elif what == "qk":
                        act.wait_ge(qk_done, at(f, 4, n + 1))
                        if n == 2:
                            act.wait_ge(qk_stored[2], at(f, N_QS, 0))
                        copy(QK_OUT[n][:, 0, :], LIN_BANK[n][:]).then_inc(qk_high, 1)
                    elif what == "v":
                        act.wait_ge(v_prod, at(f, TT, n + 1))
                        if n:
                            act.wait_ge(v_done, at(f, TT, n))
                        elif m is not None:
                            act.wait_ge(v_done, at(m, TT, TT))
                        copy(VC[:], LIN_BANK[(n + 2) % 4][:, D:2 * D]).then_inc(v_half, 1)
                    elif what == "sc":
                        for q in range(4):
                            u = 4 * n + q
                            w = (S, W1)[q % 2]
                            dst = (P0, P1)[q % 2][:, n % 2, 2 * (q // 2):2 * (q // 2) + 2, :]
                            act.wait_ge(st_done, at(m, N_S, u + 1))
                            if q == 0:
                                act.wait_ge(av_done, at(m, N_G, max(0, n - 1)))
                                if n < 2 and f is not None:
                                    act.wait_ge(qk_stored[n], at(f, N_QS, N_QS))
                            nc.scalar.activation(dst, S_BANK[u % 2][:, 0:2 * w].rearrange("p (a i) -> p a i", a=2),
                                                 ACT.Exp, scale=SCALE).then_inc(exp_done, 1)
                    elif what == "av":
                        act.wait_ge(av_done, at(m, N_G, n + 1))
                        if n == 0:
                            act.wait_ge(o_turned, at(m, TT, 0))
                        elif n == NG:
                            act.wait_ge(o_turned, at(m, TT, 2))
                        elif n == 2:
                            for s in range(SEQS):
                                act.wait_ge(m_loaded[s], at(m, N_M, N_M))
                        copy(OT[:, n % NG, :], AV_BANK[:, 0:S]).then_inc(ot_done, 1)
                    elif what == "on":
                        act.wait_ge(on_turned, at(m, SEQS, n + 1))
                        if n == 0 and b is not None:
                            act.wait_ge(gu_prod, at(b, 2 * IB, 2 * IB))
                        copy(seq(YT, 0, n), TURN_KT).then_inc(on_high, 1)
                    elif what == "z2":
                        act.wait_ge(z2_turned, at(c, SEQS, n + 1))
                        act.wait_ge(wo_prod, at(c, TT, 2 * n + 2))
                        copy(seq(YT, 0, n), TURN_KT).then_inc(z2_high, 1)
                    elif what == "gu" and n % 2 == 0:
                        ib = n // 2
                        act.wait_ge(gu_prod, at(b, 2 * IB, n + 1))
                        act.wait_ge(in_low, at(b, IB, max(0, ib - 1)))
                        nc.scalar.activation(GU[:, ib % 2, :], LIN_BANK[n % 4][:], ACT.Tanh, scale=0.5).then_inc(tanh_done, 1)
                    elif what == "gu":
                        ib = n // 2
                        act.wait_ge(up_done, at(b, IB, ib + 1))
                        if ib == 0:
                            act.wait_ge(dn_prod, at(b, TT, 0))
                        copy(IN[:, ib, 0, :], GU[:, ib % 2, :]).then_inc(in_high, 1)
            run(act, turn)

        @block.vector
        def _(dve):
            tt = nc.vector.tensor_tensor
            ts = nc.vector.tensor_scalar
            stt = nc.vector.scalar_tensor_tensor
            coefs, cubics = [0], [0]

            def low(dst, src, high):
                return tt(dst, src, high.bitcast(F32), ALU.subtract)

            def turn(steps, b, m, f):
                whole = steps in (FIRST_TURN, STARTUP, LAST_TURN, BACK_ONLY)
                step = [0]

                def own(i):
                    step[0] += 1
                    i.then_inc(step_done, 1)
                    if whole:
                        dve.wait_ge(step_done, 1 + base[0] + step[0])
                    else:
                        dve.wait_ge(step_done, f[0] * N_STEP + (1 + base[0] - N_STEP + step[0]))

                def coef(i):
                    coefs[0] += 1
                    i.then_inc(coef_done, 1)
                    dve.wait_ge(coef_done, coefs[0])

                def cubic(i):
                    cubics[0] += 1
                    i.then_inc(cubic_done, 1)
                    dve.wait_ge(cubic_done, cubics[0])

                def residual(j, done):
                    own(tt(X1[:, j, :], X1[:, j, :], LIN_BANK[j][:, D:2 * D], ALU.add))
                    tt(X1[:, j, :], X1[:, j, :], LIN_BANK[j][:, 0:D], ALU.add).then_inc(done, 1)

                for what, n in steps:
                    c = b if (what, n) in LATE else m
                    if what == "raw":
                        dve.wait_ge(raw_high, 3)
                        low(WQKl[:], raw(0, 2), WQKh[:]).then_inc(raw_low, 1)
                        low(WV[:, :, D:2 * D], raw(2, 1), WV[:, :, 0:D]).then_inc(raw_low, 1)
                        low(WO[:, :, D:2 * D], raw(3, 1), WO[:, :, 0:D]).then_inc(raw_low, 1)
                    elif what == "co":
                        dve.wait_ge(points_loaded, 2 * DMA)
                        p0, p1, p2, p3 = (CP[:, :, i, :] for i in range(4))
                        a1, a2, a3 = (CO[:, :, i, :] for i in range(3))
                        coef(tt(a1, p2, p0, ALU.subtract))
                        coef(stt(out=CT[:], in0=p1, scalar=-5.0, in1=p3, op0=ALU.mult, op1=ALU.subtract))
                        coef(stt(out=CT[:], in0=p2, scalar=4.0, in1=CT[:], op0=ALU.mult, op1=ALU.add))
                        coef(stt(out=a2, in0=p0, scalar=2.0, in1=CT[:], op0=ALU.mult, op1=ALU.add))
                        coef(stt(out=CT[:], in0=p1, scalar=3.0, in1=p0, op0=ALU.mult, op1=ALU.subtract))
                        coef(stt(out=CT[:], in0=p2, scalar=-3.0, in1=CT[:], op0=ALU.mult, op1=ALU.add))
                        coef(tt(a3, CT[:], p3, ALU.add))
                        coef(ts(CT[:], p1, 0.5, None, ALU.mult))
                    elif what == "sd":
                        dve.wait_ge(affine_done, n + 1)
                        cubic(tt(SW[:, n], SW[:, n], FR[:], ALU.mult))
                        for g in range(GI):
                            i = stt(out=SW[:, n, g, :], in0=SW[:, n, g, :], scalar=CO[:, n, 0, g:g + 1],
                                    in1=FR[:, g, :], op0=ALU.add, op1=ALU.mult)
                        cubic(i)
                    elif what == "wt":
                        dve.wait_ge(wt_high, n + 1)
                        low(spline_part(n, 1), spline_bank(n), spline_part(n, 0)).then_inc(wt_low, 1)
                    elif what in ("ln1a", "ln2a"):
                        i, src = (0, X) if what == "ln1a" else (1, X1)
                        if what == "ln1a":
                            if n == 0:
                                dve.wait_ge(x_loaded, at(f, DMA, DMA))
                        else:
                            dve.wait_ge(x1_done, at(c, TT, 2 * n + 2))
                        js = (2 * n, 2 * n + 1)
                        for j in js:
                            last = nc.vector.bn_stats(ST[i][:, j, :], src[:, j, :])
                        own(last)
                        dve.sem_inc(bn_on, 1)
                        for j in js:
                            last = nc.vector.bn_aggr(MV[i][:, j, :], ST[i][:, j, :])
                        own(last)
                        ts(VE[i][:, js[0]:js[0] + 2], MV[i][:, js[0]:js[0] + 2, 1], EPS, None,
                           ALU.add).then_inc(var_done[i], 1)
                    elif what in ("ln1b", "ln2b"):
                        i, src, own_turn = (0, X, f) if what == "ln1b" else (1, X1, c)
                        dve.wait_ge(rstd_done[i], at(own_turn, SEQS, n + 1))
                        if what == "ln1b" and n == 0 and b is not None:
                            dve.wait_ge(z2_turned, at(b, SEQS, SEQS))
                        elif what == "ln1b" and n == 0 and m is not None:
                            dve.wait_ge(qk_stored[3], at(m, N_QS, N_QS))
                        for j in (2 * n, 2 * n + 1):
                            ts(Z[:, j, :], src[:, j, :], MV[i][:, j, 0:1], RSTD[i][:, j:j + 1],
                               ALU.subtract, ALU.mult).then_inc(rows_done[i], 1)
                    elif what == "zt":
                        dve.wait_ge(z_high, at(f, SEQS, n + 1))
                        low(seq(ZT, 1, n), TURN_KT, seq(ZT, 0, n)).then_inc(z_low, 1)
                    elif what == "qk":
                        dve.wait_ge(qk_high, at(f, 4, n + 1))
                        low(QK_OUT[n][:, 1, :], LIN_BANK[n][:], QK_OUT[n][:, 0, :]).then_inc(qk_split, 1)
                    elif what == "v":
                        dve.wait_ge(v_half, at(f, TT, n + 1))
                        if n == 0:
                            dve.wait_ge(av_done, at(f, N_G, 0))
                        tt(V[:, n, :, 0, :], LIN_BANK[(n + 2) % 4][:, 0:D].rearrange("p (h c) -> p h c", c=DH),
                           VC[:].rearrange("p (h c) -> p h c", c=DH), ALU.add).then_inc(v_done, 1)
                    elif what == "s1":
                        s, p, it = n // (2 * NP), n // 2 % NP, n % 2
                        w = (128 + AHEAD, S)[it]
                        if n == 0:
                            dve.wait_ge(mt_turned, at(m, SEQS, 0))
                        dve.wait_ge(s1_done, at(m, N_S, n + 1))
                        nc.vector.tensor_reduce(out=M[:, s, it, :].rearrange("p (a k) -> p a k", a=2)[:, :, p],
                                                in_=S_BANK[n % 2][:, 0:2 * w].rearrange("p (a j) -> p a j", a=2),
                                                axis=AX.X, op=ALU.max, negate=True).then_inc(max_done, 1)
                    elif what == "mt":
                        if n == 0:
                            dve.wait_ge(o_turned, at(m, TT, 0))
                        dve.wait_ge(mt_turned, at(m, SEQS, n + 1))
                        nc.vector.tensor_copy(MT[:, n, :].bitcast(F32R), TURN_BANK[0:H, 0:S]).then_inc(mt_done, 1)
                    elif what == "ot":
                        dve.wait_ge(o_turned, at(m, TT, n + 1))
                        if n == 0 and f is not None:
                            dve.wait_ge(qk_stored[3], at(f, N_QS, N_QS))
                        heads = TURN_BANK[:].rearrange("p (h c) -> p h c", c=2 * DH)
                        own(nc.vector.reciprocal(R[:], heads[:, :, DH]))
                        tt(Z[:, n, :].rearrange("p (h c) -> p h c", c=DH), heads[:, :, 0:DH],
                           R[:].unsqueeze(2).broadcast_to([128, H, DH]), ALU.mult).then_inc(o_done, 1)
                    elif what == "on":
                        dve.wait_ge(on_high, at(m, SEQS, n + 1))
                        low(seq(YT, 1, n), TURN_KT, seq(YT, 0, n)).then_inc(on_low, 1)
                    elif what == "wo":
                        if n % 2 == 0:
                            dve.wait_ge(xr_loaded[n // 2], at(c, DMA, DMA))
                        dve.wait_ge(wo_prod, at(c, TT, n + 1))
                        residual(n, x1_done)
                    elif what == "z2":
                        dve.wait_ge(z2_high, at(c, SEQS, n + 1))
                        low(seq(YT, 1, n), TURN_KT, seq(YT, 0, n)).then_inc(z2_low, 1)
                    elif what == "gu" and n % 2 == 0:
                        g = GU[:, n // 2 % 2, :]
                        dve.wait_ge(tanh_done, at(b, IB, n // 2 + 1))
                        stt(out=g, in0=g, scalar=1.0, in1=LIN_BANK[n % 4][:], op0=ALU.add,
                            op1=ALU.mult).then_inc(gate_done, 1)
                    elif what == "gu":
                        g = GU[:, n // 2 % 2, :]
                        dve.wait_ge(gate_done, at(b, IB, n // 2 + 1))
                        dve.wait_ge(gu_prod, at(b, 2 * IB, n + 1))
                        tt(g, g, LIN_BANK[n % 4][:], ALU.mult).then_inc(up_done, 1)
                    elif what == "dn":
                        dve.wait_ge(dn_prod, at(b, TT, n + 1))
                        if n == 0:
                            dve.wait_ge(x1_done, at(b, TT, TT))
                        residual(n, y_done)
                if whole:
                    base[0] += step[0]
                else:
                    assert step[0] == N_STEP
                    base[0] += N_STEP * (TURNS - 2)

            base = [0]
            N_STEP = 2 * SEQS + 2 * SEQS + TT + TT + TT
            run(dve, turn)

        @block.tensor
        def _(pe):
            mm = nc.tensor.matmul
            turn_to = nc.tensor.transpose

            def turn_rows(s, done):
                for k in range(KB):
                    for it in range(2):
                        i = turn_to(TURN_BANK[:, k * S + it * 128:k * S + (it + 1) * 128],
                                    Z[:, 2 * s + it, k * 128:(k + 1) * 128], ID[:])
                i.then_inc(done, 1)

            def columns(b, wh, wl, act, done):
                for kb in range(KB):
                    mm(b[:], wh[:, kb], act[:, 0, kb, :], start=kb == 0, stop=False)
                    mm(b[:], wh[:, kb], act[:, 1, kb, :], start=False, stop=False)
                    i = mm(b[:], wl[:, kb], act[:, 0, kb, :], start=False, stop=kb == KB - 1)
                i.then_inc(done, 1)

            def rows(b, blocks, act, w, done):
                for k in range(blocks):
                    if k < blocks - 1:
                        mm(b[:], act(k, 0), w[:, k, :], start=k == 0, stop=False, skip_group_check=True)
                    mm(b[:, 0:D], act(k, 1), w[:, k, 0:D], start=False, stop=False, skip_group_check=True)
                mm(b[:], act(k, 0), w[:, k, :], start=False, stop=True, skip_group_check=True).then_inc(done, 1)

            def turn(steps, b, m, f):
                for what, n in steps:
                    c = b if (what, n) in LATE else m
                    if what == "raw":
                        pe.wait_ge(const_loaded, 3 * DMA)
                    elif what == "zt":
                        pe.wait_ge(rows_done[0], at(f, TT, 2 * n + 2))
                        if n == 1:
                            pe.wait_ge(z_low, at(f, SEQS, 1))
                        elif m is not None:
                            pe.wait_ge(mt_done, at(m, SEQS, SEQS))
                        turn_rows(n, z_turned)
                    elif what == "qk":
                        if n == 0:
                            pe.wait_ge(raw_low, 3)
                            pe.wait_ge(z_low, at(f, SEQS, SEQS))
                        if b is not None:
                            pe.wait_ge((gate_done, up_done)[n % 2], at(b, IB, (GU_BEFORE - 4 + n) // 2 + 1))
                        elif m is not None and n == 0:
                            pe.wait_ge(v_done, at(m, TT, TT))
                        cols = slice(n * 128, (n + 1) * 128)
                        columns(LIN_BANK[n], WQKh[:, :, cols], WQKl[:, :, cols], ZT, qk_done)
                    elif what == "v":
                        if m is not None and n >= 2:
                            pe.wait_ge(x1_done, at(m, TT, n - 1))
                        elif b is not None:
                            pe.wait_ge(y_done, at(b, TT, n + 3))
                        else:
                            pe.wait_ge(qk_split, at(f, 4, (n + 2) % 4 + 1))
                        rows(LIN_BANK[(n + 2) % 4], KB, lambda k, part: ZT[:, part, k, n * 128:(n + 1) * 128], WV, v_prod)
                    elif what == "s1":
                        s, p, it = n // (2 * NP), n // 2 % NP, n % 2
                        w = (128 + AHEAD, S)[it]
                        bk = S_BANK[n % 2]
                        if n == 0:
                            pe.wait_ge(zero_loaded, at(m, N_ZERO, N_ZERO))
                            pe.wait_ge(ks_loaded, at(m, N_QM, N_QM))
                            pe.wait_ge(qm_loaded, at(m, N_QM, N_QM))
                        if n < 2:
                            pe.wait_ge(exp_done, at(m, N_S, 0))
                        else:
                            pe.wait_ge(max_done, at(m, N_S, n - 1))
                        i0 = s * S + it * 128
                        for a in range(2):
                            mm(bk[:, a * w:(a + 1) * w], QM[:, p, a, i0:i0 + 128], KS[:, p, s * S:s * S + w],
                               start=a == 0, stop=False, skip_group_check=True)
                        c0 = AHEAD + it * 128
                        mm(bk[:, 0:2 * w].rearrange("p (a j) -> p a j", a=2)[:, :, c0:w], IDB[:],
                           UP[:, 0:w - c0].unsqueeze(1).broadcast_to([128, 2, w - c0]), start=False, stop=True,
                           skip_group_check=True).then_inc(s1_done, 1)
                    elif what == "mt":
                        pe.wait_ge(max_done, at(m, N_S, (n + 1) * 2 * NP))
                        if n:
                            pe.wait_ge(mt_done, at(m, SEQS, 1))
                        elif b is not None:
                            pe.wait_ge(z2_low, at(b, SEQS, SEQS))
                        else:
                            pe.wait_ge(z_low, at(m, SEQS, SEQS))
                        for it in range(2):
                            i = turn_to(TURN_BANK[0:H, it * 128:(it + 1) * 128], M[:, n, it, :], ID[:])
                        i.then_inc(mt_turned, 1)
                    elif what == "sc":
                        s = n // NG
                        if n % NG == 0:
                            pe.wait_ge(m_loaded[s], at(m, N_M, N_M))
                        for q in range(4):
                            u = 4 * n + q
                            p, jt = 2 * (n % NG) + q // 2, q % 2
                            w = (S, W1)[jt]
                            if u >= 2:
                                pe.wait_ge(exp_done, at(m, N_S, u - 1))
                            mm(S_BANK[u % 2][:, 0:2 * w], KS[:, p, s * S + jt * 128:s * S + jt * 128 + 128],
                               QM[:, p, :, s * S + (S - w):s * S + S], start=True, stop=True).then_inc(st_done, 1)
                    elif what == "av":
                        if n == 0:
                            pe.wait_ge(filled, 5)
                            pe.wait_ge(v_done, at(m, TT, TT))
                        pe.wait_ge(sel_done, at(m, 2 * N_G, 2 * n + 2))
                        pe.wait_ge(ot_done, at(m, N_G, n))
                        for jt in range(2):
                            for hl in range(4):
                                w = (S, W1)[jt]
                                i = mm(AV_BANK[32 * hl:32 * hl + 32, S - w:S], values(n // NG * 2 + jt, n % NG * 4 + hl),
                                       (P0, P1)[jt][:, n % 2, hl, :], start=jt == 0, stop=jt == 1)
                        i.then_inc(av_done, 1)
                    elif what == "ot":
                        if n == 0 and f is not None:
                            pe.wait_ge(z_low, at(f, SEQS, SEQS))
                        elif n == 0:
                            pe.wait_ge(mt_done, at(m, SEQS, SEQS))
                        elif n == 2:
                            pe.wait_ge(on_low, at(m, SEQS, 1))
                        else:
                            pe.wait_ge(o_done, at(m, TT, n))
                        if n % 2 == 0:
                            pe.wait_ge(ot_done, at(m, N_G, (n // 2 + 1) * NG))
                        for c in range(NG):
                            i = turn_to(TURN_BANK[:, c * 128:(c + 1) * 128], OT[:, c, n % 2 * 128:(n % 2 + 1) * 128], ID[:])
                        i.then_inc(o_turned, 1)
                    elif what == "on":
                        pe.wait_ge(o_done, at(m, TT, 2 * n + 2))
                        turn_rows(n, on_turned)
                    elif what == "wo":
                        if n % 2 == 0:
                            pe.wait_ge(on_low, at(c, SEQS, n // 2 + 1))
                        if n >= 2 and m is not None:
                            pe.wait_ge(v_done, at(m, TT, n - 1))
                        elif n >= 2:
                            pe.wait_ge(y_done, at((c[0] - 1, c[1]), TT, n + 1))
                        elif b is not None:
                            pe.wait_ge(y_done, at(b, TT, n + 1))
                        else:
                            pe.wait_ge(qk_split, at(f, 4, n + 1))
                        rows(LIN_BANK[n], KB, lambda k, part: YT[:, part, k, n * 128:(n + 1) * 128], WO, wo_prod)
                    elif what == "z2":
                        pe.wait_ge(rows_done[1], at(c, TT, 2 * n + 2))
                        if n == 0:
                            pe.wait_ge(on_low, at(c, SEQS, SEQS))
                        else:
                            pe.wait_ge(z2_low, at(c, SEQS, 1))
                        turn_rows(n, z2_turned)
                    elif what == "gu":
                        if n == 0:
                            pe.wait_ge(z2_low, at(b, SEQS, SEQS))
                        if n >= GU_BEFORE and f is not None:
                            pe.wait_ge(qk_split, at(f, 4, n - GU_BEFORE + 1))
                        elif n >= 4:
                            pe.wait_ge((gate_done, up_done)[n % 2], at(b, IB, n // 2 - 1))
                        elif n == 0:
                            pe.wait_ge(x1_done, at(b, TT, TT))
                            if m is not None:
                                pe.wait_ge(v_done, at(m, TT, TT))
                        cols = slice(n // 2 * 128, (n // 2 + 1) * 128)
                        columns(LIN_BANK[n % 4], WGUh[:, n % 2, :, cols], WGUl[:, n % 2, :, cols], YT, gu_prod)
                    elif what == "dn":
                        if n == 0:
                            pe.wait_ge(in_low, at(b, IB, IB))
                        pe.wait_ge((gate_done, up_done)[n % 2], at(b, IB, IB - 1 + n // 2))
                        rows(LIN_BANK[n], IB, lambda k, part: IN[:, k, part, n * 128:(n + 1) * 128], WD, dn_prod)
                    elif what == "wt":
                        if n == 0:
                            pe.wait_ge(wn_loaded, 3 * DMA)
                            pe.wait_ge(v_done, at(f, TT, TT))
                        elif n >= 4:
                            pe.wait_ge(wt_low, n - 3)
                        for q in range(4):
                            if n < 8:
                                w, kb, ob = n // 4, n // 2 % 2, n % 2 * 4 + q
                                src = WN[:, w, ob * D + kb * 128:ob * D + kb * 128 + 128]
                            else:
                                ib, hb = 2 * (n - 8) + q // 2, q % 2
                                src = WN[:, 2, hb * INTER + ib * 128:hb * INTER + ib * 128 + 128]
                            i = turn_to(LIN_BANK[n % 4][:, q * 128:(q + 1) * 128], src, ID[:])
                        i.then_inc(wt_done, 1)
                        if n == 11:
                            pe.wait_ge(wt_low, 12)
            run(pe, turn)


def kernel(L0_attn_x, L0_attn_wq, L0_attn_wk, L0_attn_wv, L0_attn_wo, L0_ffn_gate_cp, L0_ffn_up_cp,
           L0_ffn_down_cp):
    import ml_dtypes
    import concourse.bacc as bacc
    from concourse.bass_utils import run_bass_kernel_spmd

    def windows(cp):
        cp = np.asarray(cp)
        at = np.clip(np.arange(GI * 128)[None, :] + np.arange(-1, 3)[:, None], 0, NC - 1)
        return cp[at].reshape(4, GI, 128)

    points = np.stack([windows(c) for c in (L0_ffn_gate_cp, L0_ffn_up_cp, L0_ffn_down_cp)])
    arrays = {
        "x": np.asarray(L0_attn_x).reshape(B * S, D),
        "wqk": np.concatenate([np.asarray(L0_attn_wq).T, np.asarray(L0_attn_wk).T], axis=1),
        "wv": np.asarray(L0_attn_wv).T,
        "wo": np.asarray(L0_attn_wo).T,
        "points": points.transpose(3, 0, 1, 2).reshape(128, -1),
        "fractions": fraction_table(),
        "ident": np.eye(128, dtype=np.float32),
        "identb": np.eye(128, dtype=ml_dtypes.bfloat16),
        "upper": (np.triu(np.ones((128, 128)), 1) * NEG).astype(ml_dtypes.bfloat16),
    }
    arrays = {k: np.ascontiguousarray(v) for k, v in arrays.items()}
    nc = bacc.Bacc("TRN2", target_bir_lowering=False, num_devices=1)
    args = [nc.dram_tensor(k, v.shape, mybir.dt.from_np(v.dtype), kind="ExternalInput").ap()
            for k, v in arrays.items()]
    out = nc.dram_tensor("out", (B * S, D), F32, kind="ExternalOutput").ap()
    build(nc, *args, out)
    r = run_bass_kernel_spmd(nc, [arrays], core_ids=[0])
    return r.results[0]["out"].reshape(B, S, D)
```

```python
from contextlib import ExitStack

import numpy as np

import concourse.bass as bass
from concourse import mybir

F32 = mybir.dt.float32
F32R = mybir.dt.float32r
BF16 = mybir.dt.bfloat16
ALU = mybir.AluOpType
ACT = mybir.ActivationFunctionType
AX = mybir.AxisListType

B, S, D = 16, 256, 256
H, DH = 16, 16
INTER = 1024
WINDOW = 32
AHEAD = WINDOW // 2
EPS = 1e-5
SCALE = DH ** -0.5
NEG = -1e30

SEQS = 2
T = SEQS * S
TURNS = B // SEQS
TT = T // 128
KB = D // 128
IB = INTER // 128
NP = H // 2
NG = H // 4
J1 = 128 - AHEAD
W1 = S - J1
STACK = 64
MROW = 3 * DH

COMPRESSION = 128.9
NW = INTER * D
NC = max(16, int(NW / COMPRESSION))
NI = NC - 1


def spline_grid():
    t = np.linspace(0.0, NC - 1.0, NW, dtype=np.float64)
    i = np.clip(np.floor(t).astype(np.int64), 0, NC - 2)
    f = (t - i).astype(np.float32)
    first = np.searchsorted(i, np.arange(NI))
    return i, f, first, np.append(first[1:], NW) - first


GRID_I, GRID_F, FIRST, COUNT = spline_grid()
LEN = int(COUNT.min())
GI = -(-NI // 128)
assert COUNT.max() == LEN + 1


def fraction_table():
    table = np.zeros((GI * 128, LEN + 1), np.float32)
    for i in range(NI):
        table[i, :COUNT[i]] = GRID_F[FIRST[i]:FIRST[i] + COUNT[i]]
    return np.ascontiguousarray(table.reshape(GI, 128, LEN + 1).transpose(1, 0, 2)).reshape(128, -1)


def spline_runs():
    runs, i = [], 0
    while i < NI:
        n = 1
        while i + n < NI and (i + n) % 128 and FIRST[i + n] - FIRST[i] == LEN * n:
            n += 1
        runs.append((i, n))
        i += n
    return runs


N_S = SEQS * NP * 2
N_G = SEQS * NG
S1_AHEAD = 5
NORM = [("ln1a", 0), ("ln1b", 0), ("ln1a", 1), ("ln1b", 1)]
FRONT = ([("zt", 0), ("zt", 1)]
         + [("qk", i) for i in range(4)] + [("load", s) for s in range(SEQS)])
LATE = [("ot", 2), ("ot", 3), ("on", 1), ("ln2b", 0), ("xr", 1), ("wo", 2), ("wo", 3), ("z2", 0),
        ("ln2a", 1), ("ln2b", 1), ("z2", 1)]


def inner_steps(blocks):
    out = []
    for ib in range(blocks):
        out += [("gua", 2 * ib), ("gu", 2 * ib)] + ([("ic", ib - 1)] if ib else [])
        out += [("gua", 2 * ib + 1), ("gu", 2 * ib + 1)]
    return out + [("ic", blocks - 1)]


def order(back, front, norm, early=()):
    early = dict(early)

    def chosen(*steps):
        out = []
        for name in " ".join(steps).split():
            what = name.rstrip("0123456789")
            step = (what.rstrip("_"), int(name[len(what):]))
            if step in LATE or step[0] in ("gua", "gu", "ic", "dna", "dn", "y"):
                there = back
            elif step[0] in ("x", "ln1a", "ln1b"):
                there = norm
            elif step[0] in ("zt", "qk", "load") or (step[0] == "s1" and step[1] < 2 * S1_AHEAD):
                there = front
            else:
                there = True
            out += ([step] if there else []) + early.get(step, [])
        return out

    def pair(k):
        return f"s1_{2 * k} s1_{2 * k + 1}"

    steps = chosen("xr1 v0 ot2", pair(5), "v1 ot3", pair(6), "on1 v2 v3 zt0 ln2b0 wo2 wo3 zt1", pair(7),
                   "ln2a1 z2_0 qk0 ln2b1 mt0 qk1 z2_1 qk2 qk3 x0")
    parts = iter(inner_steps(IB))

    def inner(n):
        out = []
        while n:
            step = next(parts)
            out.append(step)
            n -= step[0] in ("gua", "gu")
        return " ".join(f"{what}{i}" for what, i in out)

    steps += chosen(inner(2))
    others = {3: "av0 ln1a0", 5: "av1 ln1a1", 7: "av2 ln1b0"}
    for h in range(NP):
        steps += chosen(f"sc{h}", inner((2, 2, 1, 2, 1, 2, 1, 2)[h]), pair(NP + h), inner((2, 2, 2, 1, 2, 1, 2, 1)[h]),
                        others.get(h, ""))
    steps += chosen("mt1 load0", inner(2), "av3 ln1b1", inner(2))
    steps += list(parts) if back else []
    fill = ["dna0", "", "dna1", "ot0", "dn0", "ot1 y0", "dn1", "av4 y1", "dna2", "on0", "dn2", "av5 y2 xr0", "dna3",
            "dn3", "av6 y3", ""]
    for h in range(NP, 2 * NP):
        steps += chosen(f"sc{h}", fill[2 * (h - NP)])
        if h >= 2 * NP - S1_AHEAD:
            steps += chosen(pair(h - 2 * NP + S1_AHEAD))
        steps += chosen(fill[2 * (h - NP) + 1])
    steps += chosen("load1 wo0 wo1 av7 ln2a0")
    return steps + early.get("end", [])


def back_only():
    parts = inner_steps(2 * IB)
    late = iter([("xr", 1), ("ln2b", 0), ("z2", 0), ("ot", 2), ("ot", 3), ("on", 1), ("wo", 2), ("wo", 3),
                 ("ln2a", 1), ("ln2b", 1), ("z2", 1)])
    steps = [next(late) for _ in range(4)]
    for k, step in enumerate(parts):
        steps += [step]
        if k % 5 == 1 and k < 5 * IB:
            steps += [i for i in [next(late, None)] if i]
    return steps + [(what, j) for j in range(TT) for what in ("dna", "dn", "y")]


BACK_ONLY = back_only()


def at(turn, each, n):
    t, off = turn
    return t * each + (off * each + n + 1)


def build(nc, x, wqk, wv, wo, points, fractions, ident, identb, upper, out):
    ctx = ExitStack()
    with ctx:
        def sb(name, shape, dt=F32):
            return ctx.enter_context(nc.sbuf_tensor(name, shape, dt))

        def sem(name):
            return ctx.enter_context(nc.semaphore(name))

        qk_scratch = nc.dram_tensor("qk_scratch", (2, SEQS, 2, 2, DH, NP, S), F32, kind="Internal").ap()
        w_scratch = nc.dram_tensor("w_scratch", (3, NW), F32, kind="Internal").ap()

        ID = sb("ID", [128, 128])
        IDB = sb("IDB", [128, 128], BF16)
        UP = sb("UP", [128, 128], BF16)
        WQKh = sb("WQKh", [128, KB, 2 * D], F32R)
        WQKl = sb("WQKl", [128, KB, 2 * D], F32R)
        WV = sb("WV", [128, KB, 2 * D], F32R)
        WO = sb("WO", [128, KB, 2 * D], F32R)
        WGUh = sb("WGUh", [128, 2, KB, INTER], F32R)
        WGUl = sb("WGUl", [128, 2, KB, INTER], F32R)
        WD = sb("WD", [128, IB, 2 * D], F32R)
        X = sb("X", [128, TT, D])
        X1 = sb("X1", [128, TT, D])
        Z = sb("Z", [128, TT, D])
        ST, MV, VE, RSTD = ([sb(f"{n}{i}", [128, TT] + w) for i in range(2)]
                            for n, w in (("ST", [6]), ("MV", [2]), ("VE", []), ("RSTD", [])))
        HALF = sb("HALF", [128, SEQS])
        ZT = sb("ZT", [128, 2, KB, T], F32R)
        YT = sb("YT", [128, 2, KB, T], F32R)
        QKE = sb("QKE", [128, 2, T], F32R)
        QM = sb("QM", [128, NP, 2, T], F32R)
        KS = sb("KS", [128, NP, T], F32R)
        V = sb("V", [128, TT, H, 2, DH])
        M = sb("M", [128, SEQS, 2, H])
        P0 = sb("P0", [128, 2, 4, S])
        P1 = sb("P1", [128, 2, 4, W1])
        OT = sb("OT", [128, NG, S])
        R = sb("R", [128, H])
        MT = sb("MT", [H, S])
        QK_OUT = [i.rearrange("p j d -> p (j d)").rearrange("p (a t) -> p a t", a=2).bitcast(F32R)
                  for i in (P0[:, 0, :, :], P0[:, 1, :, :], QKE[:, :, :], X[:, :, :])]

        with ExitStack() as early:
            FR = early.enter_context(nc.sbuf_tensor("FR", [128, GI, LEN + 1], F32))
            SW = early.enter_context(nc.sbuf_tensor("SW", [128, 3, GI, LEN + 1], F32))
            CP = early.enter_context(nc.sbuf_tensor("CP", [128, 3, 4, GI], F32))
            CO = early.enter_context(nc.sbuf_tensor("CO", [128, 3, 3, GI], F32))
            CT = early.enter_context(nc.sbuf_tensor("CT", [128, 3, GI], F32))
        WN = SW[:, :, :, :].rearrange("p m g s -> p (m g s)")[:, 0:3 * 2 * INTER].rearrange(
            "p (m c) -> p m c", m=3)
        GU = sb("GU", [128, 2, T])
        IN = sb("IN", [128, IB, 2, T], F32R)
        RAW = P0[:, :, :, :].rearrange("p a b c -> p (a b c)")

        bank = [ctx.enter_context(nc.psum_tensor(f"bank{i}", [128, 512], F32)) for i in range(8)]
        S_BANK = bank[0:2]
        AV_BANK = bank[2]
        TURN_BANK = bank[3]
        LIN_BANK = bank[4:8]
        TURN_KT = TURN_BANK[:].rearrange("p (k t) -> p k t", k=KB)

        const_loaded, raw_loaded, points_loaded, w_stored, w_stored_pool, wn_loaded = map(sem, (
            "const_loaded", "raw_loaded", "points_loaded", "w_stored", "w_stored_pool", "wn_loaded"))
        x_loaded = sem("x_loaded")
        xr_loaded, m_loaded, y_stored, qm_loaded, ks_loaded, zero_loaded = (
            [sem(f"{n}{s}") for s in range(SEQS)]
            for n in ("xr_loaded", "m_loaded", "y_stored", "qm_loaded", "ks_loaded", "zero_loaded"))
        qk_stored = [sem(f"qk_stored{n}") for n in range(4)]
        filled, raw_high, raw_low, coef_done, affine_done, scaled, cubic_done, spline_done, wt_done, wt_high, wt_low = map(
            sem, ("filled", "raw_high", "raw_low", "coef_done", "affine_done", "scaled", "cubic_done", "spline_done",
                  "wt_done", "wt_high", "wt_low"))
        z_turned, qk_done, v_prod, s1_done, mt_turned, st_done, av_done, o_turned, on_turned, wo_prod = map(sem, (
            "z_turned", "qk_done", "v_prod", "s1_done", "mt_turned", "st_done", "av_done", "o_turned",
            "on_turned", "wo_prod"))
        z2_turned, gu_prod, dn_prod = map(sem, ("z2_turned", "gu_prod", "dn_prod"))
        z_high, qk_high, v_done, exp_done, ot_done, on_high, z2_high, tanh_done, in_high = map(
            sem, ("z_high", "qk_high", "v_done", "exp_done", "ot_done", "on_high", "z2_high",
                  "tanh_done", "in_high"))
        step_done, z_low, qk_split, max_done, mt_done, o_done, on_low, x1_done, z2_low = map(sem, (
            "step_done", "z_low", "qk_split", "max_done", "mt_done", "o_done", "on_low", "x1_done",
            "z2_low"))
        gate_done, up_done, y_done, bn_on = map(sem, ("gate_done", "up_done", "y_done", "bn_on"))
        var_done, rstd_done, rows_done = ([sem(f"{n}{i}") for i in range(2)] for n in ("var", "rstd", "rows"))
        sel_done, in_low, pool_on = map(sem, ("sel_done", "in_low", "pool_on"))

        loop_sems = [x_loaded,
                     z_turned, qk_done, v_prod, s1_done, mt_turned, st_done, av_done, o_turned, on_turned,
                     wo_prod, z2_turned, gu_prod, dn_prod, z_high, qk_high, exp_done, ot_done, on_high,
                     z2_high, tanh_done, in_high, step_done, z_low, qk_split, v_done,
                     max_done, mt_done, o_done, on_low, x1_done, z2_low, gate_done, up_done, y_done, sel_done,
                     in_low] + var_done + rstd_done + rows_done + xr_loaded + m_loaded + y_stored + qk_stored
        loop_sems += qm_loaded + ks_loaded + zero_loaded

        DMA = 16
        N_QS, N_QM, N_ZERO, N_M = 2 * SEQS * DMA, 4 * DMA, 2 * DMA, 2 * DMA

        runs = spline_runs()
        extra = [int(i) for i in np.nonzero(COUNT == LEN + 1)[0]]
        W_PIECES = [(i, n, 0, LEN) for i, n in runs] + [(i, 1, LEN, 1) for i in extra]
        W_CHUNK = 6
        N_CHUNKS = -(-len(W_PIECES) // W_CHUNK)
        POOL_CHUNKS = (1, 3, 5)

        stores = [("ws", i) for i in range(N_CHUNKS)]
        first_maxima = [("s1", i) for i in range(2 * S1_AHEAD)]
        LOADS = [("raw", 0)] + NORM
        STARTUP = (FRONT[:2] + [("fill", 0), ("co", 0), ("split", 0), ("sa", 0)] + FRONT[2:]
                   + [("x", 0), ("sa", 1), ("sd", 0), ("sa", 2), ("sd", 1), ("sb", 0), ("sd", 2), ("sb", 1), ("sb", 2)]
                   + first_maxima + NORM + stores)
        EARLY = {("sc", h): [("wt", 3 * i + j) for j in range(3)] for i, h in enumerate((8, 9, 10, 12))}
        EARLY["sc", 0] = [("wl", 0)]
        FIRST_TURN = order(False, True, True, EARLY)
        MIDDLE_TURN = order(True, True, True)
        LAST_FRONT = order(True, True, False)
        LAST_TURN = order(True, False, False)

        def values(tile, h):
            return V[:, tile, h, :, :].rearrange("p a c -> p (a c)")

        def tokens(ib, m):
            return slice(0, T) if m is not None else slice(ib // IB * S, (ib // IB + 1) * S)

        def s1_bank(n, b):
            return LIN_BANK[n % 4] if b is None and n >= 2 * NP else S_BANK[n % 2]

        def wo_bank(n, m):
            return LIN_BANK[n] if m is not None or n < 2 else S_BANK[n - 2]

        def spline_bank(u):
            b = LIN_BANK[u % 4][:, :]
            return b if u < 8 else b.rearrange("p (a n) -> p a n", a=2)

        def spline_part(u, part):
            if u < 8:
                m, kb, half = u // 4, u // 2 % 2, u % 2
                return (WGUh, WGUl)[part][:, m, kb, half * 512:(half + 1) * 512]
            ib = 2 * (u - 8)
            return WD[:, ib:ib + 2, part * D:(part + 1) * D]

        def seq(buf, part, s):
            return buf[:, part, :, s * S:(s + 1) * S]

        def raw(i, n):
            return RAW[:, i * KB * D:(i + n) * KB * D].rearrange("p (k c) -> p k c", k=KB)

        def run(eng, turn):
            turn(LOADS, None, None, None, (0, 0))
            turn(STARTUP, None, None, (0, 0), (0, 1))
            turn(FIRST_TURN, None, (0, 0), (0, 1), (0, 2))
            with eng.Fori(1, TURNS - 2) as t:
                turn(MIDDLE_TURN, (t, -1), (t, 0), (t, 1), (t, 2))
            turn(LAST_FRONT, (TURNS - 3, 0), (TURNS - 2, 0), (TURNS - 1, 0), None)
            turn(LAST_TURN, (TURNS - 2, 0), (TURNS - 1, 0), None, None)
            turn(BACK_ONLY, (TURNS - 1, 0), None, None, None)

        block = ctx.enter_context(nc.Block())

        def store(queue, n, done):
            for i, k, a, w in W_PIECES[n * W_CHUNK:(n + 1) * W_CHUNK]:
                column, p = divmod(i, 128)
                c = int(FIRST[i]) + a
                queue.dma_start(w_scratch[:, c:c + k * w].rearrange("m (p s) -> p m s", s=w),
                                SW[p:p + k, :, column, a:a + w], allow_slow_non_contiguous=w == 1).then_inc(done, DMA)


        @block.sync
        def _(sp):
            def rows_of(dram, turn, s=None):
                t, off = turn
                first, n = (0, T) if s is None else (s * S, S)
                if isinstance(t, int):
                    a = (t + off) * T + first
                    v = dram[a:a + n, :]
                else:
                    v = dram[bass.ds(t * T + (off * T + first), n), :]
                return v.rearrange("(j p) d -> p j d", p=128)

            def turn(steps, b, m, f, g):
                for what, n in steps:
                    c = b if (what, n) in LATE else m
                    if what == "raw":
                        sp.dma_start(X[:], rows_of(x, (0, 0))).then_inc(x_loaded, DMA)
                        for dst, src in ((ID, ident), (IDB, identb), (UP, upper)):
                            sp.dma_start(dst[:], src).then_inc(const_loaded, DMA)
                        for i, k, w in ((0, 2, wqk), (2, 1, wv), (3, 1, wo)):
                            sp.dma_start(raw(i, k), w.rearrange("(k p) c -> p k c", p=128)).then_inc(raw_loaded, DMA)
                        sp.dma_start(CP[:], points.rearrange("p (m k g) -> p m k g", m=3, k=4)).then_inc(points_loaded, DMA)
                        sp.dma_start(FR[:], fractions.rearrange("p (g s) -> p g s", g=GI)).then_inc(points_loaded, DMA)
                    elif what == "x":
                        sp.wait_ge(qk_stored[3], at(g, N_QS, 0))
                        sp.dma_start(X[:], rows_of(x, g)).then_inc(x_loaded, DMA)
                    elif what == "mt":
                        sp.wait_ge(mt_done, at(m, SEQS, n + 1))
                        for a in range(2):
                            r = STACK * a + MROW
                            sp.dma_start(QM[r:r + 1, :, a, n * S:(n + 1) * S].bitcast(F32),
                                         MT[a * NP:(a + 1) * NP, :]).then_inc(m_loaded[n], DMA)
                    elif what == "qk":
                        sp.wait_ge(qk_split, at(f, 4, n + 1))
                        w, half = divmod(n, 2)
                        for s in range(SEQS):
                            for part in range(2):
                                sp.dma_start(qk_scratch[w, s, part, :, :, half * 4:half * 4 + 4, :].rearrange(
                                    "a d p t -> p (a d) t"), QK_OUT[n][:, part, s * S:(s + 1) * S].bitcast(F32)
                                ).then_inc(qk_stored[n], DMA)
                    elif what == "load":
                        if m is not None:
                            sp.wait_ge(st_done, at(m, N_S, (n + 1) * 2 * NP))
                        else:
                            sp.wait_ge(filled, 4)
                        tokens = slice(n * S, (n + 1) * S)
                        for a in range(2):
                            r, z = STACK * a + MROW, STACK * (1 - a)
                            sp.dma_start(QM[r:r + 1, :, a, tokens].bitcast(F32),
                                         QM[z:z + 1, :, a, tokens].bitcast(F32)).then_inc(zero_loaded[n], DMA)
                        if n == 0:
                            for i in range(4):
                                sp.wait_ge(qk_stored[i], at(f, N_QS, N_QS))
                        for a in range(2):
                            r = STACK * a
                            q, k = qk_scratch[0, n, :, a], qk_scratch[1, n, :, a]
                            sp.dma_start(QM[r:r + 2 * DH, :, a, tokens].bitcast(F32), q).then_inc(qm_loaded[n], DMA)
                            sp.dma_start(QM[r + 2 * DH:r + 3 * DH, :, a, tokens].bitcast(F32), q[0]).then_inc(qm_loaded[n], DMA)
                            sp.dma_start(KS[r:r + DH, :, tokens].bitcast(F32), k[0]).then_inc(ks_loaded[n], DMA)
                            sp.dma_start(KS[r + DH:r + 3 * DH, :, tokens].bitcast(F32), k).then_inc(ks_loaded[n], DMA)
                    elif what == "y" and n % 2:
                        s = n // 2
                        sp.wait_ge(y_done, at(b, TT, n + 1))
                        sp.dma_start(rows_of(out, b, s), X1[:, 2 * s:2 * s + 2, :]).then_inc(y_stored[s], DMA)
                    elif what == "xr":
                        if n == 1:
                            sp.wait_ge(y_stored[n], at(c, DMA, 0))
                        elif b is not None:
                            sp.wait_ge(y_stored[n], at(b, DMA, DMA))
                        sp.dma_start(X1[:, 2 * n:2 * n + 2, :], rows_of(x, c, n)).then_inc(xr_loaded[n], DMA)
                    elif what == "ws" and n not in POOL_CHUNKS:
                        sp.wait_ge(spline_done, 3)
                        store(sp, n, w_stored)
                    elif what == "wl":
                        pooled = sum(len(W_PIECES[i * W_CHUNK:(i + 1) * W_CHUNK]) for i in POOL_CHUNKS)
                        sp.wait_ge(w_stored, DMA * (len(W_PIECES) - pooled))
                        sp.wait_ge(w_stored_pool, DMA * pooled)
                        for i, w in enumerate((D, D, INTER)):
                            sp.dma_start(WN[:, i, :].rearrange("p (o c) -> p o c", c=w),
                                         w_scratch[i, :].rearrange("(o p c) -> p o c", p=128, c=w)).then_inc(wn_loaded, DMA)
            for i in loop_sems:
                sp.sem_inc(i, 1)
            run(sp, turn)
            for s in range(SEQS):
                sp.wait_ge(y_stored[s], 1 + DMA * TURNS)

        @block.gpsimd
        def _(pool):
            nc.gpsimd.memset(HALF[:], -0.5).then_inc(filled, 1)
            pool.wait_ge(filled, 1)

            def turn(steps, b, m, f, g):
                for what, n in steps:
                    c = b if (what, n) in LATE else m
                    if what in ("ln1a", "ln2a"):
                        i, own = (0, g) if what == "ln1a" else (1, c)
                        j = slice(2 * n, 2 * n + 2)
                        pool.wait_ge(var_done[i], at(own, SEQS, n + 1))
                        nc.gpsimd.tensor_tensor(RSTD[i][:, j], VE[i][:, j], HALF[:], ALU.pow).then_inc(rstd_done[i], 1)
                    elif what == "sc" and n % 2:
                        k = n // 2 % 2
                        pool.wait_ge(exp_done, at(m, N_S, 2 * (n + 1)))
                        pool.sem_inc(pool_on, 1)
                        nc.gpsimd.affine_select(out=P0[:, k, :, 0:J1], in_=P0[:, k, :, 0:J1], pattern=[[0, 4], [1, J1]],
                                                compare_op=ALU.is_ge, fill=0.0, base=AHEAD,
                                                channel_multiplier=-1).then_inc(sel_done, 1)
                        nc.gpsimd.affine_select(out=P1[:, k, :, 0:128], in_=P1[:, k, :, 0:128], pattern=[[0, 4], [1, 128]],
                                                compare_op=ALU.is_ge, fill=0.0, base=J1 + AHEAD - 128,
                                                channel_multiplier=-1).then_inc(sel_done, 1)
                    elif what == "sd":
                        pool.wait_ge(affine_done, n + 1)
                        nc.gpsimd.tensor_tensor(SW[:, n], SW[:, n], FR[:], ALU.mult).then_inc(scaled, 1)
                    elif what == "fill":
                        nc.gpsimd.memset(QM[:].bitcast(F32), 0.0).then_inc(filled, 1)
                        pool.wait_ge(filled, 2)
                        nc.gpsimd.memset(KS[32:64, :, :].bitcast(F32), 1.0).then_inc(filled, 1)
                        pool.wait_ge(filled, 3)
                        nc.gpsimd.memset(KS[96:128, :, :].bitcast(F32), 1.0).then_inc(filled, 1)
                        pool.wait_ge(filled, 4)
                        nc.gpsimd.memset(V[:, :, :, 1, :], 1.0).then_inc(filled, 1)
                    elif what == "ws" and n in POOL_CHUNKS:
                        pool.wait_ge(spline_done, 3)
                        store(pool, n, w_stored_pool)
                    elif what == "ic":
                        pool.wait_ge(in_high, at(b, IB, n + 1))
                        cols = tokens(n, m)
                        nc.gpsimd.tensor_tensor(IN[:, n % IB, 1, cols], GU[:, n % 2, cols], IN[:, n % IB, 0, cols].bitcast(F32),
                                                ALU.subtract).then_inc(in_low, 1)
            run(pool, turn)

        @block.scalar
        def _(act):
            copy = lambda dst, src: nc.scalar.activation(dst, src, ACT.Copy)

            def turn(steps, b, m, f, g):
                for what, n in steps:
                    c = b if (what, n) in LATE else m
                    if what == "split":
                        act.wait_ge(raw_loaded, 3 * DMA)
                        copy(WQKh[:], raw(0, 2)).then_inc(raw_high, 1)
                        copy(WV[:, :, 0:D], raw(2, 1)).then_inc(raw_high, 1)
                        copy(WO[:, :, 0:D], raw(3, 1)).then_inc(raw_high, 1)
                    elif what == "sa":
                        if n == 0:
                            act.wait_ge(points_loaded, 2 * DMA)
                            act.wait_ge(coef_done, 8)
                        for k in range(GI):
                            i = nc.scalar.activation(SW[:, n, k, :], FR[:, k, :], ACT.Identity,
                                                     bias=CO[:, n, 1, k:k + 1], scale=CO[:, n, 2, k:k + 1])
                        i.then_inc(affine_done, 1)
                    elif what == "sb":
                        act.wait_ge(cubic_done, n + 1)
                        for k in range(GI):
                            p = CP[:, n, 1, k:k + 1] if n < 2 else CT[:, n, k:k + 1]
                            i = nc.scalar.activation(SW[:, n, k, :], SW[:, n, k, :], ACT.Identity, bias=p,
                                                     scale=0.5 if n < 2 else 0.25)
                        i.then_inc(spline_done, 1)
                    elif what == "wt":
                        act.wait_ge(wt_done, n + 1)
                        copy(spline_part(n, 0), spline_bank(n)).then_inc(wt_high, 1)
                    elif what == "zt":
                        act.wait_ge(z_turned, at(f, SEQS, n + 1))
                        if n == 0:
                            act.wait_ge(v_prod, at(f, TT, 0))
                        copy(seq(ZT, 0, n), TURN_KT).then_inc(z_high, 1)
                    elif what == "qk":
                        act.wait_ge(qk_done, at(f, 4, n + 1))
                        if n == 2:
                            act.wait_ge(qk_stored[2], at(f, N_QS, 0))
                        copy(QK_OUT[n][:, 0, :], LIN_BANK[n][:]).then_inc(qk_high, 1)
                    elif what == "v":
                        act.wait_ge(v_prod, at(m, TT, n + 1))
                        if n == 0:
                            act.wait_ge(av_done, at(m, N_G, 0))
                        copy(V[:, n, :, 0, :], LIN_BANK[(n + 2) % 4][:, 0:D].rearrange("p (h c) -> p h c", c=DH)
                             ).then_inc(v_done, 1)
                    elif what == "sc":
                        group = n // 2
                        for jt in range(2):
                            w = (S, W1)[jt]
                            dst = (P0, P1)[jt][:, group % 2, 2 * (n % 2):2 * (n % 2) + 2, :]
                            u = 2 * n + jt
                            act.wait_ge(st_done, at(m, N_S, u + 1))
                            if n % 2 == 0 and jt == 0:
                                act.wait_ge(av_done, at(m, N_G, max(0, group - 1)))
                                if group < 2 and f is not None:
                                    act.wait_ge(qk_stored[group], at(f, N_QS, N_QS))
                            nc.scalar.activation(dst, S_BANK[jt][:, 0:2 * w].rearrange("p (a i) -> p a i", a=2),
                                                 ACT.Exp, scale=SCALE).then_inc(exp_done, 1)
                    elif what == "av":
                        act.wait_ge(av_done, at(m, N_G, n + 1))
                        if n == 0:
                            act.wait_ge(o_turned, at(m, TT, 0))
                        elif n == NG:
                            act.wait_ge(o_turned, at(m, TT, 2))
                        copy(OT[:, n % NG, :], AV_BANK[:, 0:S]).then_inc(ot_done, 1)
                    elif what == "on":
                        act.wait_ge(on_turned, at(c, SEQS, n + 1))
                        if n == 0 and b is not None:
                            act.wait_ge(gu_prod, at(b, 2 * IB, 2 * IB))
                        copy(seq(YT, 0, n), TURN_KT).then_inc(on_high, 1)
                    elif what == "z2":
                        act.wait_ge(z2_turned, at(c, SEQS, n + 1))
                        act.wait_ge(wo_prod, at(c, TT, 2 * n + 2))
                        copy(seq(YT, 0, n), TURN_KT).then_inc(z2_high, 1)
                    elif what == "gu" and n % 2 == 0:
                        ib = n // 2
                        act.wait_ge(gu_prod, at(b, 2 * IB, n + 1))
                        act.wait_ge(in_low, at(b, IB, max(0, ib - 1)))
                        cols = tokens(ib, m)
                        nc.scalar.activation(GU[:, ib % 2, cols], LIN_BANK[n % 4][:, cols], ACT.Tanh,
                                             scale=0.5).then_inc(tanh_done, 1)
                    elif what == "ic":
                        act.wait_ge(up_done, at(b, IB, n + 1))
                        if n == 0:
                            act.wait_ge(dn_prod, at(b, TT, 0))
                        cols = tokens(n, m)
                        copy(IN[:, n % IB, 0, cols], GU[:, n % 2, cols]).then_inc(in_high, 1)
            run(act, turn)

        @block.vector
        def _(dve):
            tt = nc.vector.tensor_tensor
            ts = nc.vector.tensor_scalar
            stt = nc.vector.scalar_tensor_tensor
            coefs = [0]

            def low(dst, src, high):
                return tt(dst, src, high.bitcast(F32), ALU.subtract)

            def turn(steps, b, m, f, g):
                whole = steps is not MIDDLE_TURN
                step = [0]

                def own(i):
                    step[0] += 1
                    i.then_inc(step_done, 1)
                    if whole:
                        dve.wait_ge(step_done, 1 + base[0] + step[0])
                    else:
                        dve.wait_ge(step_done, f[0] * N_STEP + (1 + base[0] - N_STEP + step[0]))

                def coef(i):
                    coefs[0] += 1
                    i.then_inc(coef_done, 1)
                    dve.wait_ge(coef_done, coefs[0])

                for what, n in steps:
                    c = b if (what, n) in LATE else m
                    if what == "split":
                        dve.wait_ge(raw_high, 3)
                        low(WQKl[:], raw(0, 2), WQKh[:]).then_inc(raw_low, 1)
                        low(WV[:, :, D:2 * D], raw(2, 1), WV[:, :, 0:D]).then_inc(raw_low, 1)
                        low(WO[:, :, D:2 * D], raw(3, 1), WO[:, :, 0:D]).then_inc(raw_low, 1)
                    elif what == "co":
                        dve.wait_ge(points_loaded, 2 * DMA)
                        p0, p1, p2, p3 = (CP[:, :, i, :] for i in range(4))
                        a1, a2, a3 = (CO[:, :, i, :] for i in range(3))
                        coef(tt(a1, p2, p0, ALU.subtract))
                        coef(stt(out=CT[:], in0=p1, scalar=-5.0, in1=p3, op0=ALU.mult, op1=ALU.subtract))
                        coef(stt(out=CT[:], in0=p2, scalar=4.0, in1=CT[:], op0=ALU.mult, op1=ALU.add))
                        coef(stt(out=a2, in0=p0, scalar=2.0, in1=CT[:], op0=ALU.mult, op1=ALU.add))
                        coef(stt(out=CT[:], in0=p1, scalar=3.0, in1=p0, op0=ALU.mult, op1=ALU.subtract))
                        coef(stt(out=CT[:], in0=p2, scalar=-3.0, in1=CT[:], op0=ALU.mult, op1=ALU.add))
                        coef(tt(a3, CT[:], p3, ALU.add))
                        coef(ts(CT[:], p1, 0.5, None, ALU.mult))
                    elif what == "sd":
                        dve.wait_ge(scaled, n + 1)
                        for k in range(GI):
                            i = stt(out=SW[:, n, k, :], in0=SW[:, n, k, :], scalar=CO[:, n, 0, k:k + 1],
                                    in1=FR[:, k, :], op0=ALU.add, op1=ALU.mult)
                        i.then_inc(cubic_done, 1)
                    elif what == "wt":
                        dve.wait_ge(wt_high, n + 1)
                        low(spline_part(n, 1), spline_bank(n), spline_part(n, 0)).then_inc(wt_low, 1)
                    elif what in ("ln1a", "ln2a"):
                        i, src = (0, X) if what == "ln1a" else (1, X1)
                        if what == "ln1a":
                            if n == 0:
                                dve.wait_ge(x_loaded, at(g, DMA, DMA))
                        else:
                            dve.wait_ge(x1_done, at(c, TT, 2 * n + 2))
                        js = (2 * n, 2 * n + 1)
                        for j in js:
                            last = nc.vector.bn_stats(ST[i][:, j, :], src[:, j, :])
                        own(last)
                        dve.sem_inc(bn_on, 1)
                        for j in js:
                            last = nc.vector.bn_aggr(MV[i][:, j, :], ST[i][:, j, :])
                        own(last)
                        ts(VE[i][:, js[0]:js[0] + 2], MV[i][:, js[0]:js[0] + 2, 1], EPS, None,
                           ALU.add).then_inc(var_done[i], 1)
                    elif what in ("ln1b", "ln2b"):
                        i, src, dst, own_turn = (0, X, X, g) if what == "ln1b" else (1, X1, Z, c)
                        dve.wait_ge(rstd_done[i], at(own_turn, SEQS, n + 1))
                        for j in (2 * n, 2 * n + 1):
                            ts(dst[:, j, :], src[:, j, :], MV[i][:, j, 0:1], RSTD[i][:, j:j + 1],
                               ALU.subtract, ALU.mult).then_inc(rows_done[i], 1)
                    elif what == "zt":
                        dve.wait_ge(z_high, at(f, SEQS, n + 1))
                        low(seq(ZT, 1, n), TURN_KT, seq(ZT, 0, n)).then_inc(z_low, 1)
                    elif what == "qk":
                        dve.wait_ge(qk_high, at(f, 4, n + 1))
                        low(QK_OUT[n][:, 1, :], LIN_BANK[n][:], QK_OUT[n][:, 0, :]).then_inc(qk_split, 1)
                    elif what == "s1":
                        s, p, it = n // (2 * NP), n // 2 % NP, n % 2
                        w = (128 + AHEAD, S)[it]
                        own_turn = f if n < 2 * S1_AHEAD else m
                        if n == 0:
                            dve.wait_ge(mt_turned, at(f, SEQS, 0))
                        dve.wait_ge(s1_done, at(own_turn, N_S, n + 1))
                        nc.vector.tensor_reduce(out=M[:, s, it, :].rearrange("p (a k) -> p a k", a=2)[:, :, p],
                                                in_=s1_bank(n, b)[:, 0:2 * w].rearrange("p (a j) -> p a j", a=2),
                                                axis=AX.X, op=ALU.max, negate=True).then_inc(max_done, 1)
                    elif what == "mt":
                        if n == 0:
                            dve.wait_ge(m_loaded[1], at(m, N_M, 0))
                        else:
                            dve.wait_ge(m_loaded[0], at(m, N_M, N_M))
                        dve.wait_ge(mt_turned, at(m, SEQS, n + 1))
                        nc.vector.tensor_copy(MT[:].bitcast(F32R), TURN_BANK[0:H, 0:S]).then_inc(mt_done, 1)
                    elif what == "ot":
                        dve.wait_ge(o_turned, at(c, TT, n + 1))
                        heads = TURN_BANK[:].rearrange("p (h c) -> p h c", c=2 * DH)
                        own(nc.vector.reciprocal(R[:], heads[:, :, DH]))
                        tt(Z[:, n, :].rearrange("p (h c) -> p h c", c=DH), heads[:, :, 0:DH],
                           R[:].unsqueeze(2).broadcast_to([128, H, DH]), ALU.mult).then_inc(o_done, 1)
                    elif what == "on":
                        dve.wait_ge(on_high, at(c, SEQS, n + 1))
                        low(seq(YT, 1, n), TURN_KT, seq(YT, 0, n)).then_inc(on_low, 1)
                    elif what == "wo":
                        if n % 2 == 0:
                            dve.wait_ge(xr_loaded[n // 2], at(c, DMA, DMA))
                        dve.wait_ge(wo_prod, at(c, TT, n + 1))
                        tt(X1[:, n, :], X1[:, n, :], wo_bank(n, m)[:, 0:D], ALU.add).then_inc(x1_done, 1)
                    elif what == "z2":
                        dve.wait_ge(z2_high, at(c, SEQS, n + 1))
                        low(seq(YT, 1, n), TURN_KT, seq(YT, 0, n)).then_inc(z2_low, 1)
                    elif what == "gu" and n % 2 == 0:
                        cols = tokens(n // 2, m)
                        gu = GU[:, n // 2 % 2, cols]
                        dve.wait_ge(tanh_done, at(b, IB, n // 2 + 1))
                        stt(out=gu, in0=gu, scalar=1.0, in1=LIN_BANK[n % 4][:, cols], op0=ALU.add,
                            op1=ALU.mult).then_inc(gate_done, 1)
                    elif what == "gu":
                        cols = tokens(n // 2, m)
                        gu = GU[:, n // 2 % 2, cols]
                        dve.wait_ge(gate_done, at(b, IB, n // 2 + 1))
                        dve.wait_ge(gu_prod, at(b, 2 * IB, n + 1))
                        tt(gu, gu, LIN_BANK[n % 4][:, cols], ALU.mult).then_inc(up_done, 1)
                    elif what == "y":
                        dve.wait_ge(dn_prod, at(b, TT, n + 1))
                        if n == 0:
                            dve.wait_ge(x1_done, at(b, TT, TT))
                        tt(X1[:, n, :], X1[:, n, :], LIN_BANK[n][:, 0:D], ALU.add).then_inc(y_done, 1)
                if whole:
                    base[0] += step[0]
                else:
                    assert step[0] == N_STEP
                    base[0] += N_STEP * (TURNS - 3)

            base = [0]
            N_STEP = 2 * SEQS + 2 * SEQS + TT
            run(dve, turn)

        @block.tensor
        def _(pe):
            mm = nc.tensor.matmul
            turn_to = nc.tensor.transpose

            def turn_rows(src, s, done):
                for k in range(KB):
                    for it in range(2):
                        i = turn_to(TURN_BANK[:, k * S + it * 128:k * S + (it + 1) * 128],
                                    src[:, 2 * s + it, k * 128:(k + 1) * 128], ID[:])
                i.then_inc(done, 1)

            def columns(b, part, wh, wl, act, cols, done):
                for kb in part:
                    mm(b[:, cols], wh[:, kb], act[:, 0, kb, cols], start=kb == 0, stop=False)
                    mm(b[:, cols], wh[:, kb], act[:, 1, kb, cols], start=False, stop=False)
                    i = mm(b[:, cols], wl[:, kb], act[:, 0, kb, cols], start=False, stop=kb == KB - 1)
                if part[-1] == KB - 1:
                    i.then_inc(done, 1)

            def rows(b, blocks, part, act, w, done):
                for k in part:
                    mm(b[:, 0:D], act(k, 0), w[:, k, 0:D], start=k == 0, stop=False)
                    mm(b[:, 0:D], act(k, 0), w[:, k, D:2 * D], start=False, stop=False)
                    i = mm(b[:, 0:D], act(k, 1), w[:, k, 0:D], start=False, stop=k == blocks - 1)
                if part[-1] == blocks - 1:
                    i.then_inc(done, 1)

            def turn(steps, b, m, f, g):
                for what, n in steps:
                    c = b if (what, n) in LATE else m
                    if what == "raw":
                        pe.wait_ge(const_loaded, 3 * DMA)
                    elif what == "zt":
                        pe.wait_ge(rows_done[0], at(f, TT, 2 * n + 2))
                        if n == 1:
                            pe.wait_ge(z_low, at(f, SEQS, 1))
                        elif b is not None:
                            pe.wait_ge(on_low, at(b, SEQS, SEQS))
                        elif m is not None:
                            pe.wait_ge(z_low, at(m, SEQS, SEQS))
                        turn_rows(X, n, z_turned)
                    elif what == "qk":
                        if n == 0:
                            pe.wait_ge(raw_low, 3)
                            pe.wait_ge(z_low, at(f, SEQS, SEQS))
                        if n >= 2 and b is not None:
                            pe.wait_ge(x1_done, at(b, TT, n + 1))
                        elif m is not None and n == 0:
                            pe.wait_ge(v_done, at(m, TT, TT))
                        cols = slice(n * 128, (n + 1) * 128)
                        columns(LIN_BANK[n], range(KB), WQKh[:, :, cols], WQKl[:, :, cols], ZT, slice(0, T), qk_done)
                    elif what == "v":
                        if b is None:
                            pe.wait_ge(qk_split, at(m, 4, (n + 2) % 4 + 1))
                        elif n == 0:
                            pe.wait_ge(x1_done, at(b, TT, 2))
                        rows(LIN_BANK[(n + 2) % 4], KB, range(KB), lambda k, part: ZT[:, part, k, n * 128:(n + 1) * 128],
                             WV, v_prod)
                    elif what == "s1":
                        s, p, it = n // (2 * NP), n // 2 % NP, n % 2
                        w = (128 + AHEAD, S)[it]
                        bk = s1_bank(n, b)
                        own_turn = f if n < 2 * S1_AHEAD else m
                        if p == 0 and it == 0:
                            pe.wait_ge(zero_loaded[s], at(own_turn, N_ZERO, N_ZERO))
                            pe.wait_ge(ks_loaded[s], at(own_turn, N_QM, N_QM))
                            pe.wait_ge(qm_loaded[s], at(own_turn, N_QM, N_QM))
                        if n < 2 * S1_AHEAD and m is not None:
                            pe.wait_ge(exp_done, at(m, N_S, N_S - 2 * S1_AHEAD + n + 1))
                        elif 2 <= n < 2 * NP:
                            pe.wait_ge(max_done, at(own_turn, N_S, n - 1))
                        elif 2 * NP <= n < 2 * NP + 4 and b is None:
                            pe.wait_ge(qk_split, at(f, 4, n - 2 * NP + 1))
                        elif n >= 2 * NP and b is None:
                            pe.wait_ge(max_done, at(m, N_S, n - 3))
                        elif n >= 2 * NP:
                            pe.wait_ge(exp_done, at(m, N_S, n - 2 * NP + 1))
                        i0 = s * S + it * 128
                        for a in range(2):
                            mm(bk[:, a * w:(a + 1) * w], QM[:, p, a, i0:i0 + 128], KS[:, p, s * S:s * S + w],
                               start=a == 0, stop=False, skip_group_check=True)
                        c0 = AHEAD + it * 128
                        mm(bk[:, 0:2 * w].rearrange("p (a j) -> p a j", a=2)[:, :, c0:w], IDB[:],
                           UP[:, 0:w - c0].unsqueeze(1).broadcast_to([128, 2, w - c0]), start=False, stop=True,
                           skip_group_check=True).then_inc(s1_done, 1)
                    elif what == "mt":
                        pe.wait_ge(max_done, at(m, N_S, (n + 1) * 2 * NP))
                        if n == 0 and b is not None:
                            pe.wait_ge(z2_low, at(b, SEQS, 1))
                        elif n == 0:
                            pe.wait_ge(z_low, at(f, SEQS, SEQS))
                        elif b is not None:
                            pe.wait_ge(z2_low, at(b, SEQS, SEQS))
                        else:
                            pe.wait_ge(mt_done, at(m, SEQS, 1))
                        for it in range(2):
                            i = turn_to(TURN_BANK[0:H, it * 128:(it + 1) * 128], M[:, n, it, :], ID[:])
                        i.then_inc(mt_turned, 1)
                    elif what == "sc":
                        s, p = divmod(n, NP)
                        if p == 0:
                            pe.wait_ge(m_loaded[s], at(m, N_M, N_M))
                        for jt in range(2):
                            u = 2 * n + jt
                            w = (S, W1)[jt]
                            if n == 0 or (n <= NP and b is not None):
                                pe.wait_ge(max_done, at(m, N_S, 2 * NP + u - 1))
                            elif f is not None and n > 2 * NP - S1_AHEAD:
                                pe.wait_ge(max_done, at(f, N_S, u - 1 - N_S + 2 * S1_AHEAD))
                            else:
                                pe.wait_ge(exp_done, at(m, N_S, u - 1))
                            mm(S_BANK[jt][:, 0:2 * w], KS[:, p, s * S + jt * 128:s * S + jt * 128 + 128],
                               QM[:, p, :, s * S + (S - w):s * S + S], start=True, stop=True).then_inc(st_done, 1)
                    elif what == "av":
                        if n == 0:
                            pe.wait_ge(filled, 5)
                            pe.wait_ge(v_done, at(m, TT, TT))
                        pe.wait_ge(sel_done, at(m, 2 * N_G, 2 * n + 2))
                        pe.wait_ge(ot_done, at(m, N_G, n))
                        for jt in range(2):
                            for hl in range(4):
                                w = (S, W1)[jt]
                                i = mm(AV_BANK[32 * hl:32 * hl + 32, S - w:S], values(n // NG * 2 + jt, n % NG * 4 + hl),
                                       (P0, P1)[jt][:, n % 2, hl, :], start=jt == 0, stop=jt == 1)
                        i.then_inc(av_done, 1)
                    elif what == "ot":
                        if n == 0:
                            pe.wait_ge(mt_done, at(m, SEQS, SEQS))
                        elif n == 2 and m is None:
                            pe.wait_ge(z2_low, at(c, SEQS, 1))
                        elif n == 2:
                            pe.wait_ge(on_low, at(c, SEQS, 1))
                        else:
                            pe.wait_ge(o_done, at(c, TT, n))
                        if n % 2 == 0:
                            pe.wait_ge(ot_done, at(c, N_G, (n // 2 + 1) * NG))
                        for g4 in range(NG):
                            i = turn_to(TURN_BANK[:, g4 * 128:(g4 + 1) * 128],
                                        OT[:, g4, n % 2 * 128:(n % 2 + 1) * 128], ID[:])
                        i.then_inc(o_turned, 1)
                    elif what == "on":
                        pe.wait_ge(o_done, at(c, TT, 2 * n + 2))
                        turn_rows(Z, n, on_turned)
                    elif what == "wo":
                        if n % 2 == 0:
                            pe.wait_ge(on_low, at(c, SEQS, n // 2 + 1))
                        if n >= 2 and m is not None:
                            pe.wait_ge(v_done, at(m, TT, n - 1))
                        elif n >= 2:
                            pe.wait_ge(exp_done, at(c, N_S, N_S))
                        elif b is not None:
                            pe.wait_ge(y_done, at(b, TT, n + 1))
                        else:
                            pe.wait_ge(wt_low, 12)
                        rows(wo_bank(n, m), KB, range(KB), lambda k, part: YT[:, part, k, n * 128:(n + 1) * 128], WO, wo_prod)
                    elif what == "z2":
                        pe.wait_ge(rows_done[1], at(c, TT, 2 * n + 2))
                        if n == 0 and f is not None:
                            pe.wait_ge(z_low, at(f, SEQS, SEQS))
                        elif n == 0:
                            pe.wait_ge(on_low, at(c, SEQS, SEQS if m is not None else 1))
                        elif m is not None:
                            pe.wait_ge(mt_done, at(m, SEQS, 1))
                        else:
                            pe.wait_ge(on_low, at(c, SEQS, SEQS))
                        turn_rows(Z, n, z2_turned)
                    elif what in ("gua", "gu"):
                        if n == 0:
                            pe.wait_ge(z2_low, at(b, SEQS, SEQS if m is not None else 1))
                        elif n == 2 * IB:
                            pe.wait_ge(z2_low, at(b, SEQS, SEQS))
                        if what == "gua" and n >= 4:
                            pe.wait_ge((gate_done, up_done)[n % 2], at(b, IB, n // 2 - 1))
                        elif what == "gua" and f is not None:
                            pe.wait_ge(qk_split, at(f, 4, n + 1))
                        elif what == "gua" and n == 0:
                            pe.wait_ge(x1_done, at(b, TT, TT if m is not None else 2))
                            if m is not None:
                                pe.wait_ge(v_done, at(m, TT, TT))
                        inner = slice(n // 2 % IB * 128, (n // 2 % IB + 1) * 128)
                        columns(LIN_BANK[n % 4], (0,) if what == "gua" else (1,), WGUh[:, n % 2, :, inner],
                                WGUl[:, n % 2, :, inner], YT, tokens(n // 2, m), gu_prod)
                    elif what in ("dna", "dn"):
                        if what == "dna":
                            pe.wait_ge((gate_done, up_done)[n % 2], at(b, IB, (IB if m is not None else 2 * IB) - 1 + n // 2))
                        if n == 0 or (n == 2 and m is None):
                            pe.wait_ge(in_low, at(b, IB, n // 2 * IB + (IB // 2 if what == "dna" else IB)))
                        rows(LIN_BANK[n], IB, range(IB // 2) if what == "dna" else range(IB // 2, IB),
                             lambda k, part: IN[:, k, part, n * 128:(n + 1) * 128], WD, dn_prod)
                    elif what == "wt":
                        if n == 0:
                            pe.wait_ge(wn_loaded, 3 * DMA)
                            pe.wait_ge(max_done, at(m, N_S, N_S))
                        elif n >= 4:
                            pe.wait_ge(wt_low, n - 3)
                        for q in range(4):
                            if n < 8:
                                w, kb, ob = n // 4, n // 2 % 2, n % 2 * 4 + q
                                src = WN[:, w, ob * D + kb * 128:ob * D + kb * 128 + 128]
                            else:
                                ib, hb = 2 * (n - 8) + q // 2, q % 2
                                src = WN[:, 2, hb * INTER + ib * 128:hb * INTER + ib * 128 + 128]
                            i = turn_to(LIN_BANK[n % 4][:, q * 128:(q + 1) * 128], src, ID[:])
                        i.then_inc(wt_done, 1)
            run(pe, turn)


def kernel(L0_attn_x, L0_attn_wq, L0_attn_wk, L0_attn_wv, L0_attn_wo, L0_ffn_gate_cp, L0_ffn_up_cp,
           L0_ffn_down_cp):
    import ml_dtypes
    import concourse.bacc as bacc
    from concourse.bass_utils import run_bass_kernel_spmd

    def windows(cp):
        cp = np.asarray(cp)
        at = np.clip(np.arange(GI * 128)[None, :] + np.arange(-1, 3)[:, None], 0, NC - 1)
        return cp[at].reshape(4, GI, 128)

    points = np.stack([windows(c) for c in (L0_ffn_gate_cp, L0_ffn_up_cp, L0_ffn_down_cp)])
    arrays = {
        "x": np.asarray(L0_attn_x).reshape(B * S, D),
        "wqk": np.concatenate([np.asarray(L0_attn_wq).T, np.asarray(L0_attn_wk).T], axis=1),
        "wv": np.asarray(L0_attn_wv).T,
        "wo": np.asarray(L0_attn_wo).T,
        "points": points.transpose(3, 0, 1, 2).reshape(128, -1),
        "fractions": fraction_table(),
        "ident": np.eye(128, dtype=np.float32),
        "identb": np.eye(128, dtype=ml_dtypes.bfloat16),
        "upper": (np.triu(np.ones((128, 128)), 1) * NEG).astype(ml_dtypes.bfloat16),
    }
    arrays = {k: np.ascontiguousarray(v) for k, v in arrays.items()}
    nc = bacc.Bacc("TRN2", target_bir_lowering=False, num_devices=1)
    args = [nc.dram_tensor(k, v.shape, mybir.dt.from_np(v.dtype), kind="ExternalInput").ap()
            for k, v in arrays.items()]
    out = nc.dram_tensor("out", (B * S, D), F32, kind="ExternalOutput").ap()
    build(nc, *args, out)
    r = run_bass_kernel_spmd(nc, [arrays], core_ids=[0])
    return r.results[0]["out"].reshape(B, S, D)
```
